# Optimizing a Trainium2 kernel written in Bass

```python
import numpy as np
import jax
import jax.numpy as jnp

def _softmax(x, axis=-1):
    return jax.nn.softmax(x, axis=axis)

def _gelu(x):
    return jax.nn.gelu(x, approximate=True)

def _silu(x):
    return jax.nn.silu(x)

def _sigmoid(x):
    return jax.nn.sigmoid(x)

def _layernorm(x, axis=-1, eps=1e-05):
    m = jnp.mean(x, axis=axis, keepdims=True)
    v = jnp.var(x, axis=axis, keepdims=True)
    return (x - m) / jnp.sqrt(v + eps)

def _scatter_add(tgt, idx, src, axis=0):
    return tgt.at[idx].add(src)

def _segment_sum(src, seg, n):
    return jax.ops.segment_sum(src, seg, n)
kernel_name = 'mk_cond_resid_d2_seqx_r4_1a945f'

def setup_inputs(seed: int=0):
    np.random.seed(seed)
    _w = jnp.asarray

    def _rec_inputs():
        import jax
        import jax.numpy as jnp
        _rk = jax.random.key(seed)
        x = -7.109e-05 + 0.9999 * jax.random.normal(jax.random.fold_in(_rk, 1), (32, 256, 256), jnp.float32)
        _lenS = 256 - jax.random.randint(jax.random.fold_in(_rk, 7), (32,), 0, max(1, 256 // 4) + 1, jnp.int32)
        _lenS2 = 256 - jax.random.randint(jax.random.fold_in(_rk, 8), (32,), 0, max(1, 256 // 4) + 1, jnp.int32)
        itok_B_0_3 = jax.random.randint(jax.random.fold_in(_rk, 11), (32,), 0, 4, jnp.int32)
        itok_B_0_2 = jax.random.randint(jax.random.fold_in(_rk, 12), (32,), 0, 3, jnp.int32)
        return (x, itok_B_0_3, itok_B_0_2)
    x, itok_B_0_3, itok_B_0_2 = _rec_inputs()

    def _L0_cond_setup():
        import jax, jax.numpy as jnp
        import numpy as np
        D = 256
        RANK = 16
        ALPHA = 16.0
        SCALING = ALPHA / RANK
        N_LANG = 4
        B, S = (32, 512)
        key = jax.random.key(seed)
        k1, k2, k3, k4, k5 = jax.random.split(key, 5)
        x = jax.random.normal(k1, (B, S, D), dtype=jnp.float32)
        language_ids = jax.random.randint(k2, (B,), 0, N_LANG, dtype=jnp.int32)
        lora_A = jax.random.normal(k3, (N_LANG, RANK, D), dtype=jnp.float32) * 0.02
        lora_B = jax.random.normal(k4, (N_LANG, D, RANK), dtype=jnp.float32) * 0.02
        lang_embed = jax.random.normal(k5, (N_LANG, D), dtype=jnp.float32) * 0.02
        return {'x': x, 'language_ids': language_ids, 'lora_A': lora_A, 'lora_B': lora_B, 'lang_embed': lang_embed}
    _L0_cond_all = _L0_cond_setup()
    _L0_cond_in = {k: v for k, v in _L0_cond_all.items() if k in ('lora_A', 'lora_B', 'lang_embed')}
    del _L0_cond_all

    def _L1_cond_setup():
        import jax, jax.numpy as jnp
        import numpy as np
        NEG_INF = -1e+30
        key = jax.random.key(seed)
        k1, k2, k3, k4, k5 = jax.random.split(key, 5)
        B, S, D, A = (16, 256, 256, 64)
        hidden = jax.random.normal(k1, (B, S, D), dtype=jnp.float32)
        W1 = jax.random.normal(k2, (D, A), dtype=jnp.float32) / np.sqrt(D)
        b1 = jax.random.normal(k3, (A,), dtype=jnp.float32) * 0.01
        v = jax.random.normal(k4, (A,), dtype=jnp.float32) / np.sqrt(A)
        prompt_type_ids = jax.random.randint(k5, (B,), 0, 3, dtype=jnp.int32)
        return {'hidden': hidden, 'W1': W1, 'b1': b1, 'v': v, 'prompt_type_ids': prompt_type_ids}
    _L1_cond_all = _L1_cond_setup()
    _L1_cond_in = {k: v for k, v in _L1_cond_all.items() if k in ('W1', 'b1', 'v')}
    del _L1_cond_all
    return {'x': x, 'itok_B_0_3': itok_B_0_3, 'itok_B_0_2': itok_B_0_2, 'L0_cond_lora_A': _L0_cond_in['lora_A'], 'L0_cond_lora_B': _L0_cond_in['lora_B'], 'L0_cond_lang_embed': _L0_cond_in['lang_embed'], 'L1_cond_W1': _L1_cond_in['W1'], 'L1_cond_b1': _L1_cond_in['b1'], 'L1_cond_v': _L1_cond_in['v']}

def reference(x, itok_B_0_3, itok_B_0_2, L0_cond_lora_A, L0_cond_lora_B, L0_cond_lang_embed, L1_cond_W1, L1_cond_b1, L1_cond_v):
    import jax
    import jax.numpy as jnp

    def _L0_cond_ref(x, language_ids, lora_A, lora_B, lang_embed):
        import jax, jax.numpy as jnp
        import numpy as np
        D = 256
        RANK = 16
        ALPHA = 16.0
        SCALING = ALPHA / RANK
        N_LANG = 4
        B, S = (32, 512)
        A = lora_A[language_ids]
        Bm = lora_B[language_ids]
        emb = lang_embed[language_ids]
        t = jnp.einsum('bsd,brd->bsr', x, A)
        lora_out = jnp.einsum('bsr,bdr->bsd', t, Bm) * SCALING
        return lora_out + emb[:, None, :]

    def _L1_cond_ref(hidden, W1, b1, v, prompt_type_ids):
        import jax, jax.numpy as jnp
        import numpy as np
        NEG_INF = -1e+30
        B, S, D = hidden.shape
        attn_in = jnp.tanh(jnp.einsum('bsd,da->bsa', hidden, W1) + b1)
        scores = jnp.einsum('bsa,a->bs', attn_in, v)
        idx = jnp.arange(S)
        j = idx[:, None]
        l = idx[None, :]
        prefix_m = l <= j
        postfix_m = l >= j
        cloze_m = l != j
        pt = prompt_type_ids[:, None, None]
        mask = jnp.where(pt == 0, prefix_m[None], jnp.where(pt == 1, postfix_m[None], cloze_m[None]))
        masked_scores = jnp.where(mask, scores[:, None, :], NEG_INF)
        p = jax.nn.softmax(masked_scores, axis=-1)
        cnt = jnp.sum(mask, axis=-1).astype(hidden.dtype)
        pooled = jnp.einsum('bjl,bld->bjd', p, hidden) / cnt[..., None]
        return pooled
    x = x + _L0_cond_ref(x, itok_B_0_3, L0_cond_lora_A, L0_cond_lora_B, L0_cond_lang_embed)
    x = x + _L1_cond_ref(x, L1_cond_W1, L1_cond_b1, L1_cond_v, itok_B_0_2)
    return x

_drawn_inputs = setup_inputs


def setup_inputs(seed=0):
    import zlib

    import numpy as np

    out = dict(_drawn_inputs(seed))
    spreads = {}
    factors = {'L0_cond_lang_embed': 2.87, 'L1_cond_W1': 4.349, 'L1_cond_b1': 8.0, 'L1_cond_v': 4.502}
    for name, (base, spread) in spreads.items():
        noise = np.random.default_rng([zlib.crc32(name.encode()), seed]).standard_normal(out[name].shape)
        drawn = base * np.exp(spread * noise) if base else spread * noise
        out[name] = jnp.asarray(drawn.astype(out[name].dtype))
    for name, factor in factors.items():
        out[name] = (out[name] * factor).astype(out[name].dtype)
    return out
```

```python
import concourse.bass as bass
from concourse import mybir
from contextlib import ExitStack


def lora_prompt_pool_kernel(
    nc: bass.Bass,
    x: bass.AP,
    prompt_type: bass.AP,
    language: bass.AP,
    lora_A: bass.AP,
    lora_B: bass.AP,
    lang_embed: bass.AP,
    W1: bass.AP,
    b1: bass.AP,
    v: bass.AP,
    out: bass.AP,
):
    fp32 = mybir.dt.float32
    bf16 = mybir.dt.bfloat16
    i32 = mybir.dt.int32
    ALU = mybir.AluOpType
    ACT = mybir.ActivationFunctionType

    B, S, D = x.shape
    L, R, _ = lora_A.shape
    A = W1.shape[1]
    P = 128
    NS = S // P
    ND = D // P
    NT = 3
    U = 4
    STEPS = B // U
    T0 = A
    M = A + R
    DZ = D + 1
    NEG = -1e30
    LOWEST = -3e38

    x_v = x.rearrange("b (c p) d -> b p c d", p=P)
    out_v = out.rearrange("b (c p) d -> b p c d", p=P)

    ctx = ExitStack()
    with ctx:
        def sb(name, shape, dt=fp32):
            return ctx.enter_context(nc.sbuf_tensor(name, shape, dt))

        def sem(name):
            return ctx.enter_context(nc.semaphore(name))

        x_in = sb("x_in", [P, U, NS, D])
        x1 = sb("x1", [P, B, NS, DZ + 1])
        xT = sb("xT", [P, 2, ND, S])
        tanh = sb("tanh", [A, 2, S])
        tT = sb("tT", [P, 2, S])
        pT = sb("pT", [P, 2, NS, S])
        o = sb("o", [P, U, NS, D])
        wall = sb("wall", [P, L, ND * M + D])
        wsel = sb("wsel", [P, 2, ND * M + D])
        mask = sb("mask", [P, NT, NS, S], bf16)
        pick = sb("pick", [P, B, P], bf16)
        ident = sb("ident", [P, P])
        identb = sb("identb", [P, P], bf16)
        ones = sb("ones", [P, P])
        lA = sb("lA", [R, L, D])
        lAn = sb("lAn", [L * R, D])
        lB = sb("lB", [P, L, ND, R])
        w1 = sb("w1", [P, ND, A])
        G = sb("G", [R, L, A])
        b1r = sb("b1r", [1, A])
        v_sb = sb("v_sb", [A, 1])
        emb = sb("emb", [L, D])
        embT = sb("embT", [P, ND, L])
        biasL = sb("biasL", [L, A])
        bias = sb("bias", [A, B])
        ids_i = sb("ids_i", [P, 2, B], i32)
        ids = sb("ids", [P, 2, B])
        lang_hot = sb("lang_hot", [L, B])
        part = sb("part", [P, 1])
        cnt_t = sb("cnt_t", [P, NT, NS])
        cnt = sb("cnt", [P, B, NS])
        hot = sb("hot", [P, NT, B])
        type_i = sb("type_i", [B, 1], i32)
        type_r = sb("type_r", [B, 1])
        hot_r = sb("hot_r", [B, NT])
        s_col = sb("s_col", [P, NS, B])
        s_row = sb("s_row", [B, S])
        pre = sb("pre", [B, S + 1])
        suf = sb("suf", [B, S + 1])
        m = sb("m", [B, 2, S])
        parts = sb("parts", [P, S], bf16)
        zc = sb("zc", [P, 2, NS])
        rz = sb("rz", [P, 2, NS])

        bank = [ctx.enter_context(nc.psum_tensor(f"bank{i}", [P, 512], fp32)) for i in range(8)]
        xT_ps = [bank[0], bank[1]]
        proj_ps = [bank[2], bank[3]]
        lora_ps = [bank[4], bank[5]]
        score_ps = bank[6]
        work_ps = bank[7]
        arg_ps = [bank[0], bank[1]]
        pool_ps = [[bank[2], bank[3]], [bank[4], bank[5]]]

        loaded_w = sem("loaded_w")
        consts = sem("consts")
        wall_zero = sem("wall_zero")
        link_d = sem("link_d")
        setup_pe = sem("setup_pe")
        setup_dve = sem("setup_dve")
        x_loaded = [sem(f"x_loaded{u}") for u in range(U)]
        transposed = sem("transposed")
        xT_ready = sem("xT_ready")
        w_selected = sem("w_selected")
        projected = sem("projected")
        tanh_ready = sem("tanh_ready")
        t_ready = sem("t_ready")
        lora_done = sem("lora_done")
        scored = sem("scored")
        x1_ready = sem("x1_ready")
        s_col_ready = sem("s_col_ready")
        s_row_done = sem("s_row_done")
        max_ready = sem("max_ready")
        arg_ready = sem("arg_ready")
        p_ready = sem("p_ready")
        pooled = sem("pooled")
        o_ready = sem("o_ready")
        stored = [sem(f"stored{u}") for u in range(U)]

        NW = 11
        block = ctx.enter_context(nc.Block())

        def over(eng, body):
            for u in range(U):
                body(0, u)
            with eng.Fori(1, STEPS - 1) as i:
                for u in range(U):
                    body(i, u)
            for u in range(U):
                body(STEPS - 1, u)

        @block.sync
        def _(sp):
            def load(i, u):
                b = i * U + u
                if not (isinstance(i, int) and i == 0):
                    sp.wait_ge(x1_ready, b - U + 1)
                sp.dma_start(x_in[:, u, :, :], x_v[bass.ds(b, 1), :, :, :].rearrange("b p c d -> (b p) c d")
                             ).then_inc(x_loaded[u], 16)

            over(sp, load)

            def store(i, u):
                b = i * U + u
                sp.wait_ge(o_ready, b + 1)
                sp.dma_start(out_v[bass.ds(b, 1), :, :, :].rearrange("b p c d -> (b p) c d"), o[:, u, :, :]
                             ).then_inc(stored[u], 16)

            over(sp, store)
            for u in range(U):
                sp.wait_ge(stored[u], 16 * STEPS)

        @block.gpsimd
        def _(pool):
            chain = [0]

            def did(ins):
                chain[0] += 1
                ins.then_inc(consts, 1)

            did(nc.gpsimd.memset(ones[:], 1.0))
            did(nc.gpsimd.memset(pick[:], 0.0))
            did(nc.gpsimd.memset(mask[:], 0.0))
            did(nc.gpsimd.memset(identb[:], 0.0))
            pool.wait_ge(consts, chain[0])
            did(nc.gpsimd.affine_select(out=ident[:], in_=ones[:], compare_op=ALU.is_equal, fill=0.0, base=0,
                                        pattern=[[-1, P]], channel_multiplier=1))
            did(nc.gpsimd.affine_select(out=identb[:], in_=ones[:], compare_op=ALU.is_equal, fill=0.0, base=0,
                                        pattern=[[-1, P]], channel_multiplier=1))
            for c in range(NS):
                did(nc.gpsimd.affine_select(out=mask[:, 0, c, :], in_=mask[:, 0, c, :], compare_op=ALU.is_ge, fill=NEG,
                                            base=-c * P, pattern=[[1, S]], channel_multiplier=-1))
                did(nc.gpsimd.affine_select(out=mask[:, 1, c, :], in_=mask[:, 1, c, :], compare_op=ALU.is_ge, fill=NEG,
                                            base=c * P, pattern=[[-1, S]], channel_multiplier=1))
                did(nc.gpsimd.affine_select(out=mask[:, 2, c, :], in_=mask[:, 2, c, :], compare_op=ALU.not_equal,
                                            fill=NEG, base=c * P, pattern=[[-1, S]], channel_multiplier=1))
            first = nc.gpsimd.affine_select(out=pick[:], in_=pick[:], compare_op=ALU.not_equal, fill=-1.0, base=0,
                                            pattern=[[-1, B], [0, P]], channel_multiplier=1)
            did(first)
            pool.wait_ge(consts, chain[0])
            did(nc.gpsimd.affine_select(out=pick[:], in_=pick[:], compare_op=ALU.not_equal, fill=-1.0, base=-B,
                                        pattern=[[-1, B], [0, P]], channel_multiplier=1))
            did(nc.gpsimd.iota(part[:], pattern=[[0, 1]], base=0, channel_multiplier=1,
                               allow_small_or_imprecise_dtypes=True))
            for c in range(NS):
                did(nc.gpsimd.iota(cnt_t[:, 0, c:c + 1], pattern=[[0, 1]], base=c * P + 1, channel_multiplier=1,
                                   allow_small_or_imprecise_dtypes=True))
                did(nc.gpsimd.iota(cnt_t[:, 1, c:c + 1], pattern=[[0, 1]], base=S - c * P, channel_multiplier=-1,
                                   allow_small_or_imprecise_dtypes=True))
                did(nc.gpsimd.iota(cnt_t[:, 2, c:c + 1], pattern=[[0, 1]], base=S - 1, channel_multiplier=0,
                                   allow_small_or_imprecise_dtypes=True))
            did(nc.gpsimd.memset(x1[:, :, :, D:DZ], 1.0))
            did(nc.gpsimd.memset(parts[:], 0.0))
            assert chain[0] == NCONST
            pool.wait_ge(consts, NCONST)

            def select(i, u):
                b = i * U + u
                lang = pool.value_load(ids_i[0:1, 0, bass.ds(b, 1)], min_val=0, max_val=L - 1)
                if not (isinstance(i, int) and i == 0 and u < 2):
                    pool.wait_ge(lora_done, b - 1)
                nc.gpsimd.tensor_copy(wsel[:, u % 2, :], wall[:, bass.ds(lang, 1), :].rearrange("p a n -> p (a n)")
                                      ).then_inc(w_selected, 1)

            pool.wait_ge(loaded_w, 16 * NW)
            pool.wait_ge(setup_dve, SETUP_DVE)
            over(pool, select)

        @block.tensor
        def _(pe):
            pe.wait_ge(loaded_w, 16 * NW)
            pe.wait_ge(consts, NCONST)
            W = work_ps
            for c in range(ND):
                last = nc.tensor.transpose(W[:, 64 * c:64 * c + L * R], lAn[:, c * P:(c + 1) * P], ident[0:L * R, 0:L * R])
            for c in range(ND):
                last = nc.tensor.transpose(W[:, 128 + L * c:128 + L * (c + 1)], emb[:, c * P:(c + 1) * P], ident[0:L, 0:L])
            for l in range(L):
                for c in range(ND):
                    last = nc.tensor.matmul(W[0:R, 192 + A * l:192 + A * (l + 1)], lB[:, l, c, :], w1[:, c, :],
                                            start=(c == 0), stop=(c == ND - 1))
            last.then_inc(setup_pe, 1)
            for l in range(L):
                for c in range(ND):
                    last = nc.tensor.transpose(bank[l // 2][0:R, (l % 2) * D + c * P:(l % 2) * D + (c + 1) * P],
                                               lB[:, l, c, :], ident[:])
            last.then_inc(setup_pe, 1)
            pe.wait_ge(setup_dve, 1)
            for l in range(L):
                for c in range(ND):
                    last = nc.tensor.matmul(bank[2][:, (l * ND + c) * A:(l * ND + c + 1) * A], lA[:, l, c * P:(c + 1) * P],
                                            G[:, l, :], start=True, stop=True)
            last.then_inc(setup_pe, 1)
            for c in range(ND):
                last = nc.tensor.matmul(bank[3][0:L, 0:A], embT[:, c, :], w1[:, c, :], start=(c == 0), stop=False)
            last = nc.tensor.matmul(bank[3][0:L, 0:A], ones[0:1, 0:L], b1r[:], start=False, stop=True)
            last.then_inc(setup_pe, 1)
            pe.wait_ge(setup_dve, SETUP_DVE)
            nc.tensor.matmul(bank[6][0:A, 0:B], biasL[:], lang_hot[:], start=True, stop=True).then_inc(setup_pe, 1)
            pe.wait_ge(setup_dve, SETUP_DVE + 1)

            def transpose(i, u):
                b = i * U + u
                pe.wait_ge(x_loaded[u], 16 * (i + 1))
                if not (isinstance(i, int) and i == 0 and u < 2):
                    pe.wait_ge(xT_ready, b - 1)
                for c in range(ND):
                    for s in range(NS):
                        last = nc.tensor.transpose(xT_ps[u % 2][:, c * S + s * P:c * S + (s + 1) * P],
                                                   x_in[:, u, s, c * P:(c + 1) * P], ident[:])
                last.then_inc(transposed, 1)

            def project(i, u):
                b = i * U + u
                pe.wait_ge(xT_ready, b + 1)
                pe.wait_ge(w_selected, b + 1)
                if not (isinstance(i, int) and i == 0 and u < 2):
                    pe.wait_ge(tanh_ready, b - 1)
                    pe.wait_ge(t_ready, b - 1)
                for c in range(ND):
                    last = nc.tensor.matmul(proj_ps[u % 2][0:M, 0:S], wsel[:, u % 2, c * M:(c + 1) * M],
                                            xT[:, u % 2, c, :], start=(c == 0), stop=(c == ND - 1))
                last.then_inc(projected, 1)

            def finish(i, u):
                b = i * U + u
                pe.wait_ge(t_ready, b + 1)
                if not (isinstance(i, int) and i == 0 and u < 2):
                    pe.wait_ge(x1_ready, b - 1)
                for s in range(NS):
                    last = nc.tensor.matmul(lora_ps[u % 2][:, s * D:(s + 1) * D], tT[T0:T0 + R + 1, u % 2, s * P:(s + 1) * P],
                                            wsel[T0:T0 + R + 1, u % 2, ND * M:ND * M + D], start=True, stop=True)
                last.then_inc(lora_done, 1)
                pe.wait_ge(tanh_ready, b + 1)
                for s in range(NS):
                    last = nc.tensor.matmul(score_ps[:, bass.ds(b * NS + s, 1)], tanh[:, u % 2, s * P:(s + 1) * P],
                                            v_sb[:], start=True, stop=True)
                last.then_inc(scored, 1)

            transpose(0, 0)

            def step(i, u):
                final = isinstance(i, int) and i == STEPS - 1 and u == U - 1
                if not final:
                    transpose(i + (u + 1) // U, (u + 1) % U)
                project(i, u)
                if not (isinstance(i, int) and i == 0 and u == 0):
                    finish(i - (u == 0), (u - 1) % U)

            over(pe, step)
            finish(STEPS - 1, U - 1)

            pe.wait_ge(s_col_ready, 1)
            for s in range(NS):
                last = nc.tensor.transpose(work_ps[0:B, s * P:(s + 1) * P], s_col[:, s, :], ident[:])
            last.then_inc(s_row_done, 1)
            pe.wait_ge(max_ready, 1)

            def argument(i, u):
                b = i * U + u
                kind = pe.value_load(ids_i[0:1, 1, bass.ds(b, 1)], min_val=0, max_val=NT - 1)
                if not (isinstance(i, int) and i == 0 and u < 2):
                    pe.wait_ge(p_ready, b - 1)
                nc.tensor.matmul(arg_ps[u % 2][:, :], identb[:],
                                 mask[:, bass.ds(kind, 1), :, :].rearrange("p a c n -> p (a c n)"),
                                 start=True, stop=False)
                for s in range(NS):
                    last = nc.tensor.matmul(arg_ps[u % 2][:, s * S:(s + 1) * S],
                                            pick[:, bass.ds(b, 1), :].rearrange("p a n -> p (a n)"),
                                            parts[:], start=False, stop=(s == NS - 1))
                last.then_inc(arg_ready, 1)

            def pool_rows(i, u):
                b = i * U + u
                pe.wait_ge(p_ready, b + 1)
                if not (isinstance(i, int) and i == 0 and u < 2):
                    pe.wait_ge(o_ready, b - 1)
                for j in range(NS):
                    for s in range(NS):
                        last = nc.tensor.matmul(pool_ps[u % 2][j][:, 0:DZ], pT[:, u % 2, s, j * P:(j + 1) * P],
                                                x1[:, bass.ds(b, 1), s, 0:DZ].rearrange("p a n -> p (a n)"),
                                                start=(s == 0), stop=(s == NS - 1))
                last.then_inc(pooled, 1)

            argument(0, 0)

            def row_step(i, u):
                final = isinstance(i, int) and i == STEPS - 1 and u == U - 1
                if not final:
                    argument(i + (u + 1) // U, (u + 1) % U)
                pool_rows(i, u)

            over(pe, row_step)

        @block.scalar
        def _(act):
            for dst, src in (
                (ids_i[:, 0, :], language.rearrange("(a n) -> a n", a=1).to_broadcast([P, B])),
                (ids_i[:, 1, :], prompt_type.rearrange("(a n) -> a n", a=1).to_broadcast([P, B])),
                (type_i[:], prompt_type.rearrange("(n a) -> n a", a=1)),
                (lAn[:], lora_A.rearrange("l r d -> (l r) d")),
                (lA[:], lora_A.rearrange("l r d -> r l d")),
                (lB[:].rearrange("p l c r -> p (l c) r"), lora_B.rearrange("l (c p) r -> p (l c) r", p=P)),
                (w1[:], W1.rearrange("(c p) a -> p c a", p=P)),
                (b1r[:], b1.rearrange("(o a) -> o a", o=1)),
                (v_sb[:], v.rearrange("(a o) -> a o", o=1)),
                (emb[:], lang_embed),
            ):
                act.dma_start(dst, src).then_inc(loaded_w, 16)
            act.wait_ge(wall_zero, 1)
            act.dma_start(wall[T0 + R:T0 + R + 1, :, ND * M:ND * M + D],
                          lang_embed.rearrange("(o l) d -> o l d", o=1)).then_inc(loaded_w, 16)
            act.wait_ge(setup_dve, SETUP_DVE + 1)

            def copy_xT(i, u):
                b = i * U + u
                act.wait_ge(transposed, b + 1)
                if not (isinstance(i, int) and i == 0 and u < 2):
                    act.wait_ge(projected, b - 1)
                nc.scalar.copy(xT[:, u % 2, :, :].rearrange("p c n -> p (c n)"), xT_ps[u % 2][:]).then_inc(xT_ready, 1)

            def do_tanh(i, u):
                b = i * U + u
                act.wait_ge(projected, b + 1)
                if not (isinstance(i, int) and i == 0 and u < 2):
                    act.wait_ge(scored, b - 1)
                nc.scalar.activation(tanh[:, u % 2, :], proj_ps[u % 2][0:A, 0:S], ACT.Tanh,
                                     bias=bias[:, bass.ds(b, 1)]).then_inc(tanh_ready, 1)

            copy_xT(0, 0)

            def step(i, u):
                final = isinstance(i, int) and i == STEPS - 1 and u == U - 1
                if not final:
                    copy_xT(i + (u + 1) // U, (u + 1) % U)
                do_tanh(i, u)

            over(act, step)

            def probs(i, u):
                b = i * U + u
                act.wait_ge(arg_ready, b + 1)
                if not (isinstance(i, int) and i == 0 and u < 2):
                    act.wait_ge(pooled, b - 1)
                for s in range(NS):
                    last = nc.scalar.activation(pT[:, u % 2, s, :], arg_ps[u % 2][:, s * S:(s + 1) * S], ACT.Exp,
                                                bias=s_col[:, s, bass.ds(b, 1)])
                last.then_inc(p_ready, 1)

            over(act, probs)

        @block.vector
        def _(dve):
            chain = [0]

            def link(ins):
                chain[0] += 1
                ins.then_inc(link_d, 1)
                dve.wait_ge(link_d, chain[0])

            W = work_ps
            nc.vector.memset(wall[:, :, ND * M:ND * M + D], 0.0).then_inc(wall_zero, 1)
            dve.wait_ge(loaded_w, 16 * NW)
            dve.wait_ge(consts, NCONST)
            link(nc.vector.memset(wsel[:], 0.0))
            link(nc.vector.memset(tT[:], 1.0))
            link(nc.vector.memset(pre[:, 0:1], LOWEST))
            link(nc.vector.memset(suf[:, S:S + 1], LOWEST))
            link(nc.vector.tensor_copy(ids[:], ids_i[:]))
            link(nc.vector.tensor_copy(type_r[:], type_i[:]))
            link(nc.vector.tensor_scalar(lang_hot[:], ids[0:L, 0, :], part[0:L, :], None, ALU.is_equal))
            for t in range(NT):
                link(nc.vector.tensor_single_scalar(hot[:, t, :], ids[:, 1, :], float(t), op=ALU.is_equal))
                link(nc.vector.tensor_single_scalar(hot_r[:, t:t + 1], type_r[:], float(t), op=ALU.is_equal))
            for c in range(NS):
                link(nc.vector.tensor_scalar(cnt[:, :, c], hot[:, 0, :], cnt_t[:, 0, c:c + 1], None, ALU.mult))
                for t in range(1, NT):
                    link(nc.vector.scalar_tensor_tensor(cnt[:, :, c], hot[:, t, :], cnt_t[:, t, c:c + 1],
                                                        cnt[:, :, c], ALU.mult, ALU.add))
            dve.wait_ge(setup_pe, 1)
            for c in range(ND):
                for l in range(L):
                    nc.vector.tensor_copy(wall[:, l, c * M + A:(c + 1) * M], W[:, 64 * c + R * l:64 * c + R * (l + 1)])
            nc.vector.tensor_copy(embT[:].rearrange("p c l -> p (c l)"), W[:, 128:128 + ND * L])
            nc.vector.tensor_copy(G[:].rearrange("r l a -> r (l a)"), W[0:R, 192:192 + L * A]).then_inc(setup_dve, 1)
            dve.wait_ge(setup_pe, 2)
            for l in range(L):
                nc.vector.tensor_copy(wall[T0:T0 + R, l, ND * M:ND * M + D], bank[l // 2][0:R, (l % 2) * D:(l % 2 + 1) * D])
            dve.wait_ge(setup_pe, 3)
            for l in range(L):
                for c in range(ND):
                    nc.vector.tensor_tensor(wall[:, l, c * M:c * M + A], bank[2][:, (l * ND + c) * A:(l * ND + c + 1) * A],
                                            w1[:, c, :], ALU.add)
            dve.wait_ge(setup_pe, 4)
            nc.vector.tensor_copy(biasL[:], bank[3][0:L, 0:A]).then_inc(setup_dve, 1)
            dve.wait_ge(setup_pe, 5)
            nc.vector.tensor_copy(bias[:], bank[6][0:A, 0:B]).then_inc(setup_dve, 1)

            def copy_t(i, u):
                b = i * U + u
                dve.wait_ge(projected, b + 1)
                if not (isinstance(i, int) and i == 0 and u < 2):
                    dve.wait_ge(lora_done, b - 1)
                nc.vector.tensor_copy(tT[T0:T0 + R, u % 2, :], proj_ps[u % 2][T0:T0 + R, 0:S]).then_inc(t_ready, 1)

            def add_lora(i, u):
                b = i * U + u
                dve.wait_ge(lora_done, b + 1)
                nc.vector.tensor_tensor(x1[:, bass.ds(b, 1), :, 0:D].rearrange("p a c d -> p (a c) d"),
                                        lora_ps[u % 2][:].rearrange("p (c d) -> p c d", c=NS),
                                        x_in[:, u, :, :], ALU.add).then_inc(x1_ready, 1)

            def step(i, u):
                copy_t(i, u)
                if not (isinstance(i, int) and i == 0 and u == 0):
                    add_lora(i - (u == 0), (u - 1) % U)

            over(dve, step)
            add_lora(STEPS - 1, U - 1)

            dve.wait_ge(scored, B)
            nc.vector.tensor_copy(s_col[:], score_ps[:, 0:B * NS].rearrange("p (b s) -> p s b", s=NS)).then_inc(s_col_ready, 1)
            dve.wait_ge(s_row_done, 1)
            link(nc.vector.tensor_copy(s_row[:], work_ps[0:B, 0:S]))
            link(nc.vector.tensor_tensor_scan(pre[:, 1:S + 1], s_row[:], s_row[:], LOWEST, ALU.max, ALU.max))
            link(nc.vector.tensor_tensor_scan(suf[:, S - 1::-1], s_row[:, ::-1], s_row[:, ::-1], LOWEST, ALU.max, ALU.max))
            link(nc.vector.tensor_tensor(m[:, 0, :], pre[:, 0:S], suf[:, 1:S + 1], ALU.max))
            link(nc.vector.tensor_scalar(m[:, 1, :], m[:, 0, :], hot_r[:, 2:3], None, ALU.mult))
            link(nc.vector.scalar_tensor_tensor(m[:, 0, :], pre[:, 1:S + 1], hot_r[:, 0:1], m[:, 1, :], ALU.mult, ALU.add))
            link(nc.vector.scalar_tensor_tensor(m[:, 1, :], suf[:, 0:S], hot_r[:, 1:2], m[:, 0, :], ALU.mult, ALU.add))
            link(nc.vector.tensor_copy(parts[0:B, :], m[:, 1, :]))
            nc.vector.tensor_tensor(parts[B:2 * B, :], m[:, 1, :], parts[0:B, :], ALU.subtract).then_inc(max_ready, 1)
            chain0 = chain[0]

            def output(i, u):
                b = i * U + u
                q = u % 2
                n = b * 2 + chain0
                dve.wait_ge(pooled, b + 1)
                for j in range(NS):
                    last = nc.vector.tensor_tensor(zc[:, q, j:j + 1], pool_ps[q][j][:, D:DZ], cnt[:, bass.ds(b, 1), j], ALU.mult)
                last.then_inc(link_d, 1)
                dve.wait_ge(link_d, n + 1)
                nc.vector.reciprocal(rz[:, q, :], zc[:, q, :]).then_inc(link_d, 1)
                dve.wait_ge(link_d, n + 2)
                if not (isinstance(i, int) and i == 0):
                    dve.wait_ge(stored[u], 16 * i)
                for j in range(NS):
                    last = nc.vector.scalar_tensor_tensor(o[:, u, j, :], pool_ps[q][j][:, 0:D], rz[:, q, j:j + 1],
                                                          x1[:, bass.ds(b, 1), j, 0:D].rearrange("p a d -> p (a d)"),
                                                          ALU.mult, ALU.add)
                last.then_inc(o_ready, 1)

            over(dve, output)


NCONST = 4 + 2 + 6 + 2 + 1 + 6 + 2
SETUP_DVE = 2

_INS = ['x', 'itok_B_0_2', 'itok_B_0_3', 'L0_cond_lora_A', 'L0_cond_lora_B', 'L0_cond_lang_embed',
        'L1_cond_W1', 'L1_cond_b1', 'L1_cond_v']


def kernel(**inputs):
    import numpy as _np
    import concourse.bacc as _bacc
    from concourse import mybir as _mybir
    from concourse.bass_utils import run_bass_kernel_spmd as _run

    nc = _bacc.Bacc("TRN2", target_bir_lowering=False, num_devices=1)
    arrays, args = {}, []
    for name in _INS:
        a = _np.ascontiguousarray(inputs[name])
        arrays[f"in_{name}"] = a
        args.append(nc.dram_tensor(f"in_{name}", a.shape, _mybir.dt.from_np(a.dtype), kind="ExternalInput").ap())
    out = nc.dram_tensor("out", inputs["x"].shape, _mybir.dt.float32, kind="ExternalOutput").ap()
    lora_prompt_pool_kernel(nc, *args, out)
    r = _run(nc, [arrays], core_ids=[0])
    return r.results[0]["out"]
```

```python
import concourse.bass as bass
from concourse import mybir
from contextlib import ExitStack


def lora_prompt_pool_kernel(
    nc: bass.Bass,
    x: bass.AP,
    prompt_type: bass.AP,
    language: bass.AP,
    lora_A: bass.AP,
    lora_B: bass.AP,
    lang_embed: bass.AP,
    W1: bass.AP,
    b1: bass.AP,
    v: bass.AP,
    out: bass.AP,
):
    fp32 = mybir.dt.float32
    bf16 = mybir.dt.bfloat16
    f32r = mybir.dt.float32r
    i32 = mybir.dt.int32
    ALU = mybir.AluOpType
    ACT = mybir.ActivationFunctionType

    B, S, D = x.shape
    L, R, _ = lora_A.shape
    A = W1.shape[1]
    P = 128
    NS = S // P
    ND = D // P
    NT = 3
    U = 8
    STEPS = B // U
    V = 4
    T0 = A
    REP = 3
    TL = T0 + (REP - 1) * R
    M = T0 + REP * R
    K = M + 2
    DZ = D + 2
    NEG = -1e30
    LOWEST = -3e38
    LOG2E = 1.4426950408889634
    ROUND = 12582912.0
    LN2_HI = 0.693359375
    LN2_LO = -2.12194440e-4
    LN2 = 0.6931471805599453
    NUDGE = 6e-5

    x_v = x.rearrange("b (c p) d -> b p c d", p=P)
    out_v = out.rearrange("b (c p) d -> b p c d", p=P)

    ctx = ExitStack()
    with ctx:
        def sb(name, shape, dt=fp32):
            return ctx.enter_context(nc.sbuf_tensor(name, shape, dt))

        def sem(name):
            return ctx.enter_context(nc.semaphore(name))

        x_in = sb("x_in", [P, U, NS, D])
        x1 = sb("x1", [P, B, NS, DZ])
        xT = sb("xT", [P, 2, ND, S])
        tanh = sb("tanh", [A, V, S])
        tT = sb("tT", [P, V, S], f32r)
        q = sb("q", [P, V, NS, S], f32r)
        y = sb("y", [P, V, NS, DZ])
        yh = sb("yh", [P, V, NS, DZ], f32r)
        yl = sb("yl", [P, V, NS, DZ], f32r)
        o = sb("o", [P, V, NS, D])
        wall = sb("wall", [P, L, ND, M])
        wallB = sb("wallB", [P, L, D])
        wsel = sb("wsel", [P, V, ND, M])
        wselB = sb("wselB", [P, V, D], f32r)
        mask = sb("mask", [P, NT, NS, S], bf16)
        pick = sb("pick", [P, B, P], bf16)
        picked = sb("picked", [P, B])
        ident = sb("ident", [P, P])
        identb = sb("identb", [P, P], bf16)
        ones = sb("ones", [P, P])
        lA = sb("lA", [R, L, D])
        lAn = sb("lAn", [L * R, D])
        lB = sb("lB", [P, L * ND, R])
        lBx = sb("lBx", [P, L * ND, P])
        hB = sb("hB", [P, L * D], f32r)
        rB = sb("rB", [P, L * D])
        w1 = sb("w1", [P, ND, A])
        G = sb("G", [R, L, A])
        b1r = sb("b1r", [1, A])
        v_sb = sb("v_sb", [A, 1])
        emb = sb("emb", [L, D])
        embT = sb("embT", [P, L, ND])
        biasL = sb("biasL", [L, A])
        bias = sb("bias", [A, B])
        ids_i = sb("ids_i", [P, 2, B], i32)
        ids = sb("ids", [P, 2, B])
        lang_hot = sb("lang_hot", [L, B])
        part = sb("part", [P, 1])
        low = sb("low", [P, 1])
        sign = sb("sign", [P, 1])
        cnt_t = sb("cnt_t", [P, NT, NS])
        cnt = sb("cnt", [P, B, NS])
        hot = sb("hot", [P, NT, B])
        type_i = sb("type_i", [B, 1], i32)
        type_r = sb("type_r", [B, 1])
        hot_r = sb("hot_r", [B, NT])
        s_col = sb("s_col", [P, NS, B])
        n_col = sb("n_col", [P, NS, B])
        f_col = sb("f_col", [P, NS, B])
        g_col = sb("g_col", [P, NS, B])
        q_bias = sb("q_bias", [P, NS, B])
        n_row = sb("n_row", [B, S])
        pre = sb("pre", [B, S + 1])
        suf = sb("suf", [B, S + 1])
        m = sb("m", [B, 2, S])
        parts = sb("parts", [P, S], bf16)
        zc = sb("zc", [P, 2, NS])
        rz = sb("rz", [P, 2, NS])

        bank = [ctx.enter_context(nc.psum_tensor(f"bank{i}", [P, 512], fp32)) for i in range(8)]
        xT_ps = [bank[0], bank[1]]
        proj_ps = [bank[2], bank[3]]
        lora_ps = [bank[4], bank[5]]
        score_ps = bank[6]
        work_ps = bank[7]
        arg_ps = [bank[0], bank[1]]
        pool_ps = [[bank[2], bank[3]], [bank[4], bank[5]]]

        core_loaded = sem("core_loaded")
        more_loaded = sem("more_loaded")
        ident_ready = sem("ident_ready")
        consts = sem("consts")
        early_dve = sem("early_dve")
        link_d = sem("link_d")
        small_T = sem("small_T")
        G_ready = sem("G_ready")
        folded = sem("folded")
        lBx_ready = sem("lBx_ready")
        B_T = sem("B_T")
        wall_ready = sem("wall_ready")
        hB_ready = sem("hB_ready")
        wallB_ready = sem("wallB_ready")
        bias_L = sem("bias_L")
        bias_ready = sem("bias_ready")
        x_loaded = [sem(f"x_loaded{u}") for u in range(U)]
        transposed = sem("transposed")
        xT_ready = sem("xT_ready")
        w_selected = sem("w_selected")
        projected = sem("projected")
        tanh_ready = sem("tanh_ready")
        th_ready = sem("th_ready")
        t_ready = sem("t_ready")
        lora_done = sem("lora_done")
        scored = sem("scored")
        x1_ready = sem("x1_ready")
        s_col_ready = sem("s_col_ready")
        s_row_done = sem("s_row_done")
        f_ready = sem("f_ready")
        g_ready = sem("g_ready")
        max_ready = sem("max_ready")
        arg_ready = sem("arg_ready")
        q_ready = sem("q_ready")
        y_ready = sem("y_ready")
        yh_ready = sem("yh_ready")
        yl_ready = sem("yl_ready")
        pooled = sem("pooled")
        o_ready = sem("o_ready")
        stored = [sem(f"stored{k}") for k in range(V)]

        N_CORE, N_MORE = 6, 4
        block = ctx.enter_context(nc.Block())

        def at(i, u, ahead):
            return i + (u + ahead) // U, (u + ahead) % U

        def exists(i, u, ahead):
            return not isinstance(i, int) or 0 <= i * U + u + ahead < B

        def reused(i, u, slots):
            return not isinstance(i, int) or i * U + u >= slots

        def over(eng, body):
            for u in range(U):
                body(0, u)
            with eng.Fori(1, STEPS - 1) as i:
                for u in range(U):
                    body(i, u)
            for u in range(U):
                body(STEPS - 1, u)

        @block.sync
        def _(sp):
            for dst, src in (
                (lAn[:], lora_A.rearrange("l r d -> (l r) d")),
                (w1[:], W1.rearrange("(c p) a -> p c a", p=P)),
            ):
                sp.dma_start(dst, src).then_inc(core_loaded, 16)

            def load(i, u):
                b = i * U + u
                if reused(i, u, U):
                    sp.wait_ge(x1_ready, b - U + 1)
                sp.dma_start(x_in[:, u, :, :], x_v[bass.ds(b, 1), :, :, :].rearrange("b p c d -> (b p) c d")
                             ).then_inc(x_loaded[u], 16)

            over(sp, load)

            def store(i, u):
                b = i * U + u
                sp.wait_ge(o_ready, b + 1)
                sp.dma_start(out_v[bass.ds(b, 1), :, :, :].rearrange("b p c d -> (b p) c d"), o[:, u % V, :, :]
                             ).then_inc(stored[u % V], 16)

            over(sp, store)
            for k in range(V):
                sp.wait_ge(stored[k], 16 * (B // V))

        @block.gpsimd
        def _(pool):
            nc.gpsimd.memset(ones[:], 1.0).then_inc(consts, 1)
            pool.wait_ge(consts, 1)
            for dst in (ident, identb):
                nc.gpsimd.affine_select(out=dst[:], in_=ones[:], compare_op=ALU.is_equal, fill=0.0, base=0,
                                        pattern=[[-1, P]], channel_multiplier=1).then_inc(ident_ready, 1)
            nc.gpsimd.iota(part[:], pattern=[[0, 1]], base=0, channel_multiplier=1,
                           allow_small_or_imprecise_dtypes=True)
            nc.gpsimd.memset(low[:], 0.0)
            nc.gpsimd.memset(mask[:], 0.0)
            nc.gpsimd.memset(parts[:], 0.0).then_inc(consts, 1)
            pool.wait_ge(consts, 2)
            nc.gpsimd.affine_select(out=low[:], in_=low[:], compare_op=ALU.not_equal, fill=1.0, base=-(K - 1),
                                    pattern=[[0, 1]], channel_multiplier=1).then_inc(consts, 1)
            pool.wait_ge(consts, 3)
            nc.gpsimd.affine_select(out=sign[:], in_=ones[:, 0:1], compare_op=ALU.is_ge, fill=0.0, base=-(T0 + R),
                                    pattern=[[0, 1]], channel_multiplier=1).then_inc(consts, 1)
            pool.wait_ge(consts, 4)
            nc.gpsimd.affine_select(out=sign[:], in_=sign[:], compare_op=ALU.is_ge, fill=0.0, base=T0 + 2 * R - 1,
                                    pattern=[[0, 1]], channel_multiplier=-1).then_inc(consts, 1)
            pool.wait_ge(consts, 5)
            nc.gpsimd.tensor_tensor(low[:], low[:], sign[:], ALU.add).then_inc(consts, 1)
            pool.wait_ge(consts, 6)
            nc.gpsimd.tensor_scalar(sign[:], low[:], -2.0, 1.0, ALU.mult, ALU.add).then_inc(consts, 1)
            for c in range(NS):
                for t, base, step in ((0, c * P + 1, 1), (1, S - c * P, -1), (2, S - 1, 0)):
                    nc.gpsimd.iota(cnt_t[:, t, c:c + 1], pattern=[[0, 1]], base=base, channel_multiplier=step,
                                   allow_small_or_imprecise_dtypes=True)
            for c in range(NS):
                for t, compare, base, step in ((0, ALU.is_ge, -c * P, 1), (1, ALU.is_ge, c * P, -1),
                                               (2, ALU.not_equal, c * P, -1)):
                    nc.gpsimd.affine_select(out=mask[:, t, c, :], in_=mask[:, t, c, :], compare_op=compare, fill=NEG,
                                            base=base, pattern=[[step, S]], channel_multiplier=-step)
            nc.gpsimd.memset(x1[:, :, :, D:DZ], 1.0).then_inc(consts, 1)

            def select(i, u):
                b = i * U + u
                lang = pool.value_load(ids_i[0:1, 0, bass.ds(b, 1)], min_val=0, max_val=L - 1)
                if reused(i, u, V):
                    pool.wait_ge(lora_done, b - V + 1)
                nc.gpsimd.tensor_copy(wsel[:, u % V, :, :], wall[:, bass.ds(lang, 1), :, :].rearrange("p a c n -> p (a c) n"))
                if isinstance(i, int) and i == 0 and u == 0:
                    pool.wait_ge(wallB_ready, 1)
                nc.gpsimd.tensor_copy(wselB[:, u % V, :], wallB[:, bass.ds(lang, 1), :].rearrange("p a n -> p (a n)")
                                      ).then_inc(w_selected, 1)

            pool.wait_ge(more_loaded, 16 * N_MORE)
            pool.wait_ge(wall_ready, 1)
            over(pool, select)

            def low_y(i, u):
                b = i * U + u
                pool.wait_ge(yh_ready, b + 1)
                if reused(i, u, V):
                    pool.wait_ge(pooled, b - V + 1)
                nc.gpsimd.tensor_tensor(yl[:, u % V, :, :], y[:, u % V, :, :], yh[:, u % V, :, :].bitcast(fp32), ALU.subtract
                                        ).then_inc(yl_ready, 1)

            over(pool, low_y)

        @block.tensor
        def _(pe):
            W = work_ps
            pe.wait_ge(core_loaded, 16 * N_CORE)
            pe.wait_ge(ident_ready, 2)
            for c in range(ND):
                nc.tensor.transpose(W[:, 64 * c:64 * c + L * R], lAn[:, c * P:(c + 1) * P], ident[0:L * R, 0:L * R])
                nc.tensor.transpose(W[:, 128 + L * c:128 + L * (c + 1)], emb[:, c * P:(c + 1) * P], ident[0:L, 0:L])
            for l in range(L):
                for c in range(ND):
                    last = nc.tensor.matmul(W[0:R, 192 + A * l:192 + A * (l + 1)], lB[:, l * ND + c, :], w1[:, c, :],
                                            start=(c == 0), stop=(c == ND - 1))
            last.then_inc(small_T, 1)
            pe.wait_ge(G_ready, 1)
            for l in range(L):
                for c in range(ND):
                    last = nc.tensor.matmul(bank[2][:, (l * ND + c) * A:(l * ND + c + 1) * A], lA[:, l, c * P:(c + 1) * P],
                                            G[:, l, :], start=True, stop=True)
            last.then_inc(folded, 1)
            pe.wait_ge(lBx_ready, 1)
            pe.wait_ge(more_loaded, 16 * N_MORE)
            for c in range(ND):
                nc.tensor.matmul(bank[3][0:L, 0:A], embT[:, :, c], w1[:, c, :], start=(c == 0), stop=False)
            nc.tensor.matmul(bank[3][0:L, 0:A], ones[0:1, 0:L], b1r[:], start=False, stop=True).then_inc(bias_L, 1)
            pe.wait_ge(lBx_ready, 1)
            for l in range(L):
                for c in range(ND):
                    last = nc.tensor.transpose(bank[4 + l // 2][:, (l % 2) * D + c * P:(l % 2) * D + (c + 1) * P],
                                               lBx[:, l * ND + c, :], ident[:])
            last.then_inc(B_T, 1)
            pe.wait_ge(bias_L, 2)
            nc.tensor.matmul(bank[6][0:A, 0:B], biasL[:], lang_hot[:], start=True, stop=True).then_inc(bias_L, 1)
            pe.wait_ge(wallB_ready, 1)
            pe.wait_ge(bias_ready, 1)

            def transpose(i, u):
                b = i * U + u
                pe.wait_ge(x_loaded[u], 16 * (i + 1))
                if reused(i, u, 2):
                    pe.wait_ge(xT_ready, b - 1)
                for c in range(ND):
                    for s in range(NS):
                        last = nc.tensor.transpose(xT_ps[u % 2][:, c * S + s * P:c * S + (s + 1) * P],
                                                   x_in[:, u, s, c * P:(c + 1) * P], ident[:])
                last.then_inc(transposed, 1)

            def project(i, u):
                b = i * U + u
                pe.wait_ge(xT_ready, b + 1)
                pe.wait_ge(w_selected, b + 1)
                if reused(i, u, 2):
                    pe.wait_ge(tanh_ready, b - 1)
                    pe.wait_ge(t_ready, b - 1)
                for c in range(ND):
                    last = nc.tensor.matmul(proj_ps[u % 2][0:M, 0:S], wsel[:, u % V, c, :],
                                            xT[:, u % 2, c, :], start=(c == 0), stop=(c == ND - 1))
                last.then_inc(projected, 1)

            def finish(i, u):
                b = i * U + u
                pe.wait_ge(t_ready, b + 1)
                if reused(i, u, 2):
                    pe.wait_ge(x1_ready, b - 1)
                for s in range(NS):
                    last = nc.tensor.matmul(lora_ps[u % 2][:, s * D:(s + 1) * D], tT[T0:K, u % V, s * P:(s + 1) * P],
                                            wselB[T0:K, u % V, :], start=True, stop=True)
                last.then_inc(lora_done, 1)
                pe.wait_ge(tanh_ready, b + 1)
                for s in range(NS):
                    last = nc.tensor.matmul(score_ps[:, bass.ds(b * NS + s, 1)], tanh[:, u % V, s * P:(s + 1) * P],
                                            v_sb[:], start=True, stop=True)
                last.then_inc(scored, 1)

            transpose(0, 0)

            def step(i, u):
                if exists(i, u, 1):
                    transpose(*at(i, u, 1))
                project(i, u)
                if exists(i, u, -2):
                    finish(*at(i, u, -2))

            over(pe, step)
            finish(STEPS - 1, U - 2)
            finish(STEPS - 1, U - 1)

            pe.wait_ge(s_col_ready, 1)
            for s in range(NS):
                last = nc.tensor.transpose(work_ps[0:B, s * P:(s + 1) * P], s_col[:, s, :], ident[:])
            last.then_inc(s_row_done, 1)
            pe.wait_ge(max_ready, 1)

            def argument(i, u):
                b = i * U + u
                kind = pe.value_load(ids_i[0:1, 1, bass.ds(b, 1)], min_val=0, max_val=NT - 1)
                if reused(i, u, 2):
                    pe.wait_ge(q_ready, b - 1)
                nc.tensor.matmul(arg_ps[u % 2][:, :], identb[:],
                                 mask[:, bass.ds(kind, 1), :, :].rearrange("p a c n -> p (a c n)"),
                                 start=True, stop=False)
                for s in range(NS):
                    last = nc.tensor.matmul(arg_ps[u % 2][:, s * S:(s + 1) * S],
                                            pick[:, bass.ds(b, 1), :].rearrange("p a n -> p (a n)"),
                                            parts[:], start=False, stop=(s == NS - 1))
                last.then_inc(arg_ready, 1)

            def pool_rows(i, u):
                b = i * U + u
                pe.wait_ge(q_ready, b + 1)
                pe.wait_ge(yl_ready, b + 1)
                if reused(i, u, 2):
                    pe.wait_ge(o_ready, b - 1)
                for j in range(NS):
                    for s in range(NS):
                        for k, part_y in enumerate((yh, yl)):
                            last = nc.tensor.matmul(pool_ps[u % 2][j][:, 0:DZ], q[:, u % V, s, j * P:(j + 1) * P],
                                                    part_y[:, u % V, s, :], start=(s + k == 0), stop=(s + k == NS))
                last.then_inc(pooled, 1)

            argument(0, 0)

            def row_step(i, u):
                if exists(i, u, 1):
                    argument(*at(i, u, 1))
                pool_rows(i, u)

            over(pe, row_step)

        @block.scalar
        def _(act):
            for dst, src in (
                (lB[:], lora_B.rearrange("l (c p) r -> p (l c) r", p=P)),
                (lA[:], lora_A.rearrange("l r d -> r l d")),
                (emb[:], lang_embed),
                (v_sb[:], v.rearrange("(a o) -> a o", o=1)),
            ):
                act.dma_start(dst, src).then_inc(core_loaded, 16)
            for dst, src in (
                (ids_i[:, 0, :], language.rearrange("(a n) -> a n", a=1).to_broadcast([P, B])),
                (b1r[:], b1.rearrange("(o a) -> o a", o=1)),
                (ids_i[:, 1, :], prompt_type.rearrange("(a n) -> a n", a=1).to_broadcast([P, B])),
                (type_i[:], prompt_type.rearrange("(n a) -> n a", a=1)),
            ):
                act.dma_start(dst, src).then_inc(more_loaded, 16)
            act.wait_ge(B_T, 1)
            for n in range(L // 2):
                last = nc.scalar.copy(hB[:, n * 2 * D:(n + 1) * 2 * D], bank[4 + n][:])
            last.then_inc(hB_ready, 1)
            act.wait_ge(bias_L, 3)
            nc.scalar.copy(bias[:], bank[6][0:A, 0:B]).then_inc(bias_ready, 1)
            act.wait_ge(bias_ready, 1)

            def copy_xT(i, u):
                b = i * U + u
                act.wait_ge(transposed, b + 1)
                if reused(i, u, 2):
                    act.wait_ge(projected, b - 1)
                nc.scalar.copy(xT[:, u % 2, :, :].rearrange("p c n -> p (c n)"), xT_ps[u % 2][:]).then_inc(xT_ready, 1)

            def narrow(i, u):
                b = i * U + u
                act.wait_ge(projected, b + 1)
                if reused(i, u, V):
                    act.wait_ge(scored, b - V + 1)
                nc.scalar.copy(tT[T0:M, u % V, :], proj_ps[u % 2][T0:M, 0:S]).then_inc(th_ready, 1)
                nc.scalar.activation(tanh[:, u % V, :], proj_ps[u % 2][0:A, 0:S], ACT.Tanh,
                                     bias=bias[:, bass.ds(b, 1)]).then_inc(tanh_ready, 1)

            copy_xT(0, 0)

            def step(i, u):
                if exists(i, u, 1):
                    copy_xT(*at(i, u, 1))
                narrow(i, u)

            over(act, step)
            act.wait_ge(f_ready, 1)
            nc.scalar.activation(g_col[:], f_col[:], ACT.Exp).then_inc(g_ready, 1)

            def high_y(i, u):
                b = i * U + u
                act.wait_ge(y_ready, b + 1)
                if reused(i, u, V):
                    act.wait_ge(pooled, b - V + 1)
                nc.scalar.copy(yh[:, u % V, :, :], y[:, u % V, :, :]).then_inc(yh_ready, 1)

            def powers(i, u):
                b = i * U + u
                act.wait_ge(arg_ready, b + 1)
                if reused(i, u, V):
                    act.wait_ge(pooled, b - V + 1)
                for s in range(NS):
                    last = nc.scalar.activation(q[:, u % V, s, :], arg_ps[u % 2][:, s * S:(s + 1) * S], ACT.Exp,
                                                bias=q_bias[:, s, bass.ds(b, 1)], scale=LN2)
                last.then_inc(q_ready, 1)

            high_y(0, 0)
            high_y(0, 1)

            def row_step(i, u):
                powers(i, u)
                if exists(i, u, 2):
                    high_y(*at(i, u, 2))

            over(act, row_step)

        @block.vector
        def _(dve):
            chain = [0]

            def link(ins):
                chain[0] += 1
                ins.then_inc(link_d, 1)
                dve.wait_ge(link_d, chain[0])

            W = work_ps
            nc.vector.memset(tT[T0:P, :, :].bitcast(fp32), 1.0)
            nc.vector.memset(pre[:, 0:1], LOWEST)
            nc.vector.memset(suf[:, S:S + 1], LOWEST)
            link(nc.vector.memset(lBx[:], 0.0))
            dve.wait_ge(ident_ready, 2)
            link(nc.vector.tensor_tensor(picked[:], ident[:, 0:B], ident[:, B:2 * B], ALU.add))
            link(nc.vector.tensor_tensor(picked[:], picked[:], ident[:, 2 * B:3 * B], ALU.add))
            nc.vector.tensor_scalar(pick[:], picked[:].rearrange("p (b a) -> p b a", a=1).to_broadcast([P, B, P]),
                                    -1.0, None, ALU.mult).then_inc(early_dve, 1)
            dve.wait_ge(small_T, 1)
            nc.vector.tensor_copy(G[:].rearrange("r l a -> r (l a)"), W[0:R, 192:192 + L * A]).then_inc(G_ready, 1)
            for k in range(REP):
                nc.vector.tensor_copy(wall[:, :, :, A + k * R:A + (k + 1) * R],
                                      W[:, 0:128].rearrange("p (c l r) -> p l c r", c=ND, l=L))
            link(nc.vector.tensor_copy(embT[:], W[:, 128:128 + ND * L].rearrange("p (c l) -> p l c", c=ND)))
            for k in range(REP):
                nc.vector.tensor_copy(lBx[:, :, T0 + k * R:T0 + (k + 1) * R], lB[:])
            nc.vector.tensor_copy(lBx[:, :, M:K], embT[:].rearrange("p l (c a) -> p (l c) a", a=1).to_broadcast([P, L * ND, 2])
                                  ).then_inc(lBx_ready, 1)
            dve.wait_ge(folded, 1)
            for l in range(L):
                last = nc.vector.tensor_tensor(wall[:, l, :, 0:A], bank[2][:, l * ND * A:(l + 1) * ND * A].rearrange("p (c a) -> p c a", c=ND),
                                               w1[:], ALU.add)
            last.then_inc(wall_ready, 1)
            dve.wait_ge(more_loaded, 16 * N_MORE)
            link(nc.vector.tensor_copy(ids[:], ids_i[:]))
            dve.wait_ge(bias_L, 1)
            nc.vector.tensor_copy(biasL[:], bank[3][0:L, 0:A])
            dve.wait_ge(consts, 8)
            nc.vector.tensor_scalar(lang_hot[:], ids[0:L, 0, :], part[0:L, :], None, ALU.is_equal).then_inc(bias_L, 1)
            dve.wait_ge(hB_ready, 1)
            for n in range(L // 2):
                part_n = slice(n * 2 * D, (n + 1) * 2 * D)
                link(nc.vector.tensor_scalar(rB[:, part_n], bank[4 + n][:], low[:], None, ALU.mult))
            nc.vector.scalar_tensor_tensor(wallB[:].rearrange("p l d -> p (l d)"), hB[:].bitcast(fp32),
                                           sign[:], rB[:], ALU.mult, ALU.add).then_inc(wallB_ready, 1)

            def low_t(i, u):
                b = i * U + u
                dve.wait_ge(th_ready, b + 1)
                nc.vector.tensor_tensor(tT[TL:M, u % V, :], proj_ps[u % 2][TL:M, 0:S], tT[TL:M, u % V, :].bitcast(fp32),
                                        ALU.subtract).then_inc(t_ready, 1)

            def add_lora(i, u):
                b = i * U + u
                dve.wait_ge(lora_done, b + 1)
                nc.vector.tensor_tensor(x1[:, bass.ds(b, 1), :, 0:D].rearrange("p a c d -> p (a c) d"),
                                        lora_ps[u % 2][:].rearrange("p (c d) -> p c d", c=NS),
                                        x_in[:, u, :, :], ALU.add).then_inc(x1_ready, 1)

            def step(i, u):
                low_t(i, u)
                if exists(i, u, -2):
                    add_lora(*at(i, u, -2))

            over(dve, step)
            add_lora(STEPS - 1, U - 2)
            add_lora(STEPS - 1, U - 1)

            dve.wait_ge(scored, B)
            nc.vector.tensor_copy(s_col[:], score_ps[:, 0:B * NS].rearrange("p (b s) -> p s b", s=NS)).then_inc(s_col_ready, 1)
            dve.wait_ge(s_col_ready, 1)
            link(nc.vector.tensor_scalar(n_col[:], s_col[:], LOG2E, ROUND, ALU.mult, ALU.add))
            link(nc.vector.tensor_scalar(n_col[:], n_col[:], ROUND, None, ALU.subtract))
            link(nc.vector.scalar_tensor_tensor(f_col[:], n_col[:], -LN2_HI, s_col[:], ALU.mult, ALU.add))
            nc.vector.scalar_tensor_tensor(f_col[:], n_col[:], -LN2_LO, f_col[:], ALU.mult, ALU.add).then_inc(f_ready, 1)
            nc.vector.tensor_scalar(q_bias[:], n_col[:], LN2, NUDGE, ALU.mult, ALU.add)
            link(nc.vector.tensor_copy(type_r[:], type_i[:]))
            for t in range(NT):
                nc.vector.tensor_single_scalar(hot[:, t, :], ids[:, 1, :], float(t), op=ALU.is_equal)
                link(nc.vector.tensor_single_scalar(hot_r[:, t:t + 1], type_r[:], float(t), op=ALU.is_equal))
            dve.wait_ge(s_row_done, 1)
            link(nc.vector.tensor_scalar(n_row[:], work_ps[0:B, 0:S], LOG2E, ROUND, ALU.mult, ALU.add))
            link(nc.vector.tensor_scalar(n_row[:], n_row[:], ROUND, None, ALU.subtract))
            link(nc.vector.tensor_tensor_scan(pre[:, 1:S + 1], n_row[:], n_row[:], LOWEST, ALU.max, ALU.max))
            link(nc.vector.tensor_tensor_scan(suf[:, S - 1::-1], n_row[:, ::-1], n_row[:, ::-1], LOWEST, ALU.max, ALU.max))
            link(nc.vector.tensor_tensor(m[:, 0, :], pre[:, 0:S], suf[:, 1:S + 1], ALU.max))
            link(nc.vector.tensor_scalar(m[:, 1, :], m[:, 0, :], hot_r[:, 2:3], None, ALU.mult))
            link(nc.vector.scalar_tensor_tensor(m[:, 0, :], pre[:, 1:S + 1], hot_r[:, 0:1], m[:, 1, :], ALU.mult, ALU.add))
            link(nc.vector.scalar_tensor_tensor(m[:, 1, :], suf[:, 0:S], hot_r[:, 1:2], m[:, 0, :], ALU.mult, ALU.add))
            link(nc.vector.tensor_copy(parts[0:B, :], m[:, 1, :]))
            link(nc.vector.tensor_tensor(m[:, 0, :], m[:, 1, :], parts[0:B, :], ALU.subtract))
            link(nc.vector.tensor_copy(parts[B:2 * B, :], m[:, 0, :]))
            link(nc.vector.tensor_copy(m[:, 1, :], parts[B:2 * B, :]))
            nc.vector.tensor_tensor(parts[2 * B:3 * B, :], m[:, 0, :], m[:, 1, :], ALU.subtract).then_inc(max_ready, 1)

            def weigh(i, u):
                b = i * U + u
                if reused(i, u, V):
                    dve.wait_ge(yl_ready, b - V + 1)
                for s in range(NS):
                    last = nc.vector.tensor_scalar(y[:, u % V, s, :], x1[:, bass.ds(b, 1), s, :].rearrange("p a d -> p (a d)"),
                                                   g_col[:, s, bass.ds(b, 1)], None, ALU.mult)
                last.then_inc(y_ready, 1)

            dve.wait_ge(g_ready, 1)
            weigh(0, 0)
            weigh(0, 1)
            for c in range(NS):
                link(nc.vector.tensor_scalar(cnt[:, :, c], hot[:, 0, :], cnt_t[:, 0, c:c + 1], None, ALU.mult))
                for t in range(1, NT):
                    link(nc.vector.scalar_tensor_tensor(cnt[:, :, c], hot[:, t, :], cnt_t[:, t, c:c + 1],
                                                        cnt[:, :, c], ALU.mult, ALU.add))
            chain0 = chain[0]

            def output(i, u):
                b = i * U + u
                k = u % 2
                n = b * 2 + chain0
                dve.wait_ge(pooled, b + 1)
                for j in range(NS):
                    last = nc.vector.tensor_tensor(zc[:, k, j:j + 1], pool_ps[k][j][:, D:D + 1], cnt[:, bass.ds(b, 1), j], ALU.mult)
                last.then_inc(link_d, 1)
                dve.wait_ge(link_d, n + 1)
                nc.vector.reciprocal(rz[:, k, :], zc[:, k, :]).then_inc(link_d, 1)
                dve.wait_ge(link_d, n + 2)
                if reused(i, u, V):
                    dve.wait_ge(stored[u % V], i * (16 * U // V) + 16 * (u // V))
                for j in range(NS):
                    last = nc.vector.scalar_tensor_tensor(o[:, u % V, j, :], pool_ps[k][j][:, 0:D], rz[:, k, j:j + 1],
                                                          x1[:, bass.ds(b, 1), j, 0:D].rearrange("p a d -> p (a d)"),
                                                          ALU.mult, ALU.add)
                last.then_inc(o_ready, 1)

            def row_step(i, u):
                if exists(i, u, 2):
                    weigh(*at(i, u, 2))
                output(i, u)

            over(dve, row_step)


_INS = ['x', 'itok_B_0_2', 'itok_B_0_3', 'L0_cond_lora_A', 'L0_cond_lora_B', 'L0_cond_lang_embed',
        'L1_cond_W1', 'L1_cond_b1', 'L1_cond_v']


def kernel(**inputs):
    import numpy as _np
    import concourse.bacc as _bacc
    from concourse import mybir as _mybir
    from concourse.bass_utils import run_bass_kernel_spmd as _run

    nc = _bacc.Bacc("TRN2", target_bir_lowering=False, num_devices=1)
    arrays, args = {}, []
    for name in _INS:
        a = _np.ascontiguousarray(inputs[name])
        arrays[f"in_{name}"] = a
        args.append(nc.dram_tensor(f"in_{name}", a.shape, _mybir.dt.from_np(a.dtype), kind="ExternalInput").ap())
    out = nc.dram_tensor("out", inputs["x"].shape, _mybir.dt.float32, kind="ExternalOutput").ap()
    lora_prompt_pool_kernel(nc, *args, out)
    r = _run(nc, [arrays], core_ids=[0])
    return r.results[0]["out"]
```

```python
import concourse.bass as bass
from concourse import mybir
from contextlib import ExitStack


def lora_prompt_pool_kernel(
    nc: bass.Bass,
    x: bass.AP,
    prompt_type: bass.AP,
    language: bass.AP,
    lora_A: bass.AP,
    lora_B: bass.AP,
    lang_embed: bass.AP,
    W1: bass.AP,
    b1: bass.AP,
    v: bass.AP,
    out: bass.AP,
):
    fp32 = mybir.dt.float32
    bf16 = mybir.dt.bfloat16
    f32r = mybir.dt.float32r
    i32 = mybir.dt.int32
    ALU = mybir.AluOpType
    ACT = mybir.ActivationFunctionType

    B, S, D = x.shape
    L, R, _ = lora_A.shape
    A = W1.shape[1]
    P = 128
    NS = S // P
    ND = D // P
    NT = 3
    U = 8
    V = 4
    T0 = A
    REP = 3
    TL = T0 + (REP - 1) * R
    M = T0 + REP * R
    K = M + 2
    DZ = D + 2
    NEG = -1e30
    BIG = 1e38
    LOG2E = 1.4426950408889634
    ROUND = 12582912.0
    LN2_HI = 0.693359375
    LN2_LO = -2.12194440e-4
    LN2 = 0.6931471805599453
    NUDGE = 6e-5

    x_v = x.rearrange("b (c p) d -> b p c d", p=P)
    out_v = out.rearrange("b (c p) d -> b p c d", p=P)

    ctx = ExitStack()
    with ctx:
        def sb(name, shape, dt=fp32):
            return ctx.enter_context(nc.sbuf_tensor(name, shape, dt))

        def sem(name):
            return ctx.enter_context(nc.semaphore(name))

        x_in = sb("x_in", [P, U, NS, D])
        x1 = sb("x1", [P, B, NS, DZ])
        xT = sb("xT", [P, 2, ND, S])
        tanh = sb("tanh", [2 * A, V, S])
        tT = sb("tT", [P, V, S], f32r)
        q = sb("q", [P, V, NS, S], f32r)
        y = sb("y", [P, V, NS, DZ])
        yh = sb("yh", [P, V, NS, DZ], f32r)
        yl = sb("yl", [P, V, NS, DZ], f32r)
        o = sb("o", [P, V, NS, D])
        wall = sb("wall", [P, L, ND, M])
        wallB = sb("wallB", [P, L, D])
        wsel = sb("wsel", [P, V, ND, M])
        wselB = sb("wselB", [P, V, D], f32r)
        mask = sb("mask", [P, NT, NS, S], bf16)
        pick = sb("pick", [P, B, P], bf16)
        picked = sb("picked", [P, B])
        ident = sb("ident", [P, P])
        identb = sb("identb", [P, P], bf16)
        ones = sb("ones", [P, P])
        spare = sb("spare", [P, 1])
        lAn = sb("lAn", [L * R, D])
        lB = sb("lB", [P, L * ND, R])
        lBx = sb("lBx", [P, L * ND, P])
        hB = sb("hB", [P, L * D], f32r)
        rB = sb("rB", [P, L * D])
        w1 = sb("w1", [P, ND, A])
        own = sb("own", [L * R, L])
        G = sb("G", [L * R, L, A])
        b1r = sb("b1r", [1, A])
        v_sb = sb("v_sb", [2 * A, 1])
        v_hot = sb("v_hot", [2 * A, B // 2, B])
        v_row = sb("v_row", [2 * A, V, B])
        emb = sb("emb", [L, D])
        embT = sb("embT", [P, ND * L])
        biasL = sb("biasL", [L, A])
        bias = sb("bias", [A, B])
        ids_i = sb("ids_i", [P, 2, B], i32)
        ids = sb("ids", [P, 2, B])
        lang_hot = sb("lang_hot", [L, B])
        part = sb("part", [P, 1])
        low = sb("low", [P, 1])
        sign = sb("sign", [P, 1])
        cnt_t = sb("cnt_t", [P, NT, NS])
        cnt = sb("cnt", [P, B, NS])
        hot = sb("hot", [P, NT, B])
        type_i = sb("type_i", [B, 1], i32)
        type_r = sb("type_r", [B, 1])
        hot_r = sb("hot_r", [B, NT])
        cap = sb("cap", [B, NT])
        s_row = sb("s_row", [B, S])
        s_col = sb("s_col", [P, NS, B])
        n_col = sb("n_col", [P, NS, B])
        f_col = sb("f_col", [P, NS, B])
        g_col = sb("g_col", [P, NS, B])
        q_bias = sb("q_bias", [P, NS, B])
        n_row = sb("n_row", [B, S])
        pre = sb("pre", [B, S + 1])
        suf = sb("suf", [B, S + 1])
        m = sb("m", [B, 2, S])
        parts = sb("parts", [P, S], bf16)
        zc = sb("zc", [P, 2, NS])
        rz = sb("rz", [P, 2, NS])

        psum = ctx.enter_context(nc.psum_tensor("psum", [P, 8, 512], fp32))
        bank = [psum[:, i, :] for i in range(8)]
        xT_ps = [bank[0], bank[1]]
        proj_ps = [bank[2], bank[3]]
        lora_ps = [bank[4], bank[5]]
        score_ps = bank[6]
        work_ps = bank[7]
        arg_ps = [bank[0], bank[1]]
        pool_ps = [psum[:, 2:4, :], psum[:, 6:8, :]]

        core_loaded = sem("core_loaded")
        v_loaded = sem("v_loaded")
        more_loaded = sem("more_loaded")
        ident_ready = sem("ident_ready")
        consts = sem("consts")
        pick_ready = sem("pick_ready")
        mask_ready = sem("mask_ready")
        link_d = sem("link_d")
        small_T = sem("small_T")
        G_ready = sem("G_ready")
        folded = sem("folded")
        lBx_ready = sem("lBx_ready")
        B_T = sem("B_T")
        wall_ready = sem("wall_ready")
        rB_ready = sem("rB_ready")
        hB_ready = sem("hB_ready")
        wallB_ready = sem("wallB_ready")
        bias_L = sem("bias_L")
        bias_ready = sem("bias_ready")
        x_loaded = [sem(f"x_loaded{u}") for u in range(U)]
        transposed = sem("transposed")
        xT_ready = sem("xT_ready")
        w_selected = sem("w_selected")
        v_selected = sem("v_selected")
        b_selected = sem("b_selected")
        projected = sem("projected")
        tanh_ready = sem("tanh_ready")
        th_ready = sem("th_ready")
        t_ready = sem("t_ready")
        lora_done = sem("lora_done")
        scored = sem("scored")
        x1_ready = sem("x1_ready")
        s_row_ready = sem("s_row_ready")
        s_col_done = sem("s_col_done")
        link_row = sem("link_row")
        link_col = sem("link_col")
        f_ready = sem("f_ready")
        g_ready = sem("g_ready")
        max_ready = sem("max_ready")
        arg_ready = sem("arg_ready")
        q_ready = sem("q_ready")
        y_odd = sem("y_odd")
        y_ready = sem("y_ready")
        yh_ready = sem("yh_ready")
        yl0_ready = sem("yl0_ready")
        yl_ready = sem("yl_ready")
        pooled = sem("pooled")
        z_ready = sem("z_ready")
        r_ready = sem("r_ready")
        o_ready = [sem(f"o_ready{j}") for j in range(NS)]
        stored = [sem(f"stored{k}") for k in range(V)]

        N_CORE, N_MORE = 5, 4
        block = ctx.enter_context(nc.Block())

        def exists(i, u):
            return not isinstance(i, int) or 0 <= i + u < B

        def reused(i, u, slots):
            return not isinstance(i, int) or i + u >= slots

        def of(t, i, u):
            if isinstance(i, int) or u < 0:
                return t[:, bass.ds(i + u, 1)]
            return t[:, u:][:, bass.ds(i, 1)]

        def over(eng, body):
            for u in range(U):
                body(0, u)
            with eng.Fori(U, B - 2 * U + 1, U) as i:
                for u in range(U):
                    body(i, u)
            for u in range(U):
                body(B - U, u)

        @block.sync
        def _(sp):
            for dst, src in (
                (lB[:, 0:L, :], lora_B[:, 0:P, :].rearrange("l p r -> p l r")),
                (lB[:, L:2 * L, :], lora_B[:, P:2 * P, :].rearrange("l p r -> p l r")),
                (w1[:], W1.rearrange("(c p) a -> p c a", p=P)),
            ):
                sp.dma_start(dst, src).then_inc(core_loaded, 16)
            for k, src in enumerate((language, prompt_type)):
                sp.dma_start(ids_i[:, k, :], src.rearrange("(a n) -> a n", a=1).to_broadcast([P, B])).then_inc(more_loaded, 16)

            def load(i, u):
                b = i + u
                if reused(i, u, U):
                    sp.wait_ge(x1_ready, b - U + 1)
                sp.dma_start(x_in[:, u % U, :, :], x_v[bass.ds(b, 1), :, :, :].rearrange("b p c d -> (b p) c d")
                             ).then_inc(x_loaded[u % U], 16)

            over(sp, load)

            def store(i, u):
                b = i + u
                if isinstance(i, int) and b == B - 1:
                    for j in range(NS):
                        sp.wait_ge(o_ready[j], B)
                        sp.dma_start(out[b, j * P:(j + 1) * P, :], o[:, u % V, j, :]).then_inc(stored[u % V], 16)
                    return
                sp.wait_ge(o_ready[NS - 1], b + 1)
                sp.dma_start(out_v[bass.ds(b, 1), :, :, :].rearrange("b p c d -> (b p) c d"), o[:, u % V, :, :]
                             ).then_inc(stored[u % V], 16)

            over(sp, store)
            for k in range(V):
                sp.wait_ge(stored[k], 16 * (B // V + (k == V - 1)))

        @block.gpsimd
        def _(pool):
            nc.gpsimd.memset(ones[:], 1.0).then_inc(consts, 1)
            pool.wait_ge(consts, 1)
            for dst in (ident, identb):
                nc.gpsimd.affine_select(out=dst[:], in_=ones[:], compare_op=ALU.is_equal, fill=0.0, base=0,
                                        pattern=[[-1, P]], channel_multiplier=1).then_inc(ident_ready, 1)
            nc.gpsimd.affine_select(out=own[:], in_=ones[0:L * R, 0:L], compare_op=ALU.is_ge, fill=0.0, base=0,
                                    pattern=[[-R, L]], channel_multiplier=1).then_inc(consts, 1)
            pool.wait_ge(consts, 2)
            nc.gpsimd.affine_select(out=own[:], in_=own[:], compare_op=ALU.is_ge, fill=0.0, base=R - 1,
                                    pattern=[[R, L]], channel_multiplier=-1).then_inc(ident_ready, 1)
            nc.gpsimd.iota(part[:], pattern=[[0, 1]], base=0, channel_multiplier=1,
                           allow_small_or_imprecise_dtypes=True)
            nc.gpsimd.memset(low[:], 0.0)
            nc.gpsimd.memset(mask[:], 0.0)
            nc.gpsimd.memset(parts[:], 0.0).then_inc(consts, 1)
            pool.wait_ge(consts, 3)
            nc.gpsimd.affine_select(out=low[:], in_=low[:], compare_op=ALU.not_equal, fill=1.0, base=-(K - 1),
                                    pattern=[[0, 1]], channel_multiplier=1).then_inc(consts, 1)
            pool.wait_ge(consts, 4)
            nc.gpsimd.affine_select(out=sign[:], in_=ones[:, 0:1], compare_op=ALU.is_ge, fill=0.0, base=-(T0 + R),
                                    pattern=[[0, 1]], channel_multiplier=1).then_inc(consts, 1)
            pool.wait_ge(consts, 5)
            nc.gpsimd.affine_select(out=sign[:], in_=sign[:], compare_op=ALU.is_ge, fill=0.0, base=T0 + 2 * R - 1,
                                    pattern=[[0, 1]], channel_multiplier=-1).then_inc(consts, 1)
            pool.wait_ge(consts, 6)
            nc.gpsimd.tensor_tensor(low[:], low[:], sign[:], ALU.add).then_inc(consts, 1)
            pool.wait_ge(consts, 7)
            nc.gpsimd.tensor_scalar(sign[:], low[:], -2.0, 1.0, ALU.mult, ALU.add).then_inc(consts, 1)
            pool.wait_ge(v_loaded, 16 * 2)
            for h in range(2):
                if h == 1:
                    pool.wait_ge(consts, 9)
                nc.gpsimd.affine_select(out=v_hot[h * A:(h + 1) * A, :, :],
                                        in_=v_sb[h * A:(h + 1) * A, :].rearrange("p (a c) -> p a c", a=1).to_broadcast([A, B // 2, B]),
                                        compare_op=ALU.is_equal, fill=0.0, base=h, pattern=[[2, B // 2], [-1, B]],
                                        channel_multiplier=0).then_inc(consts, 1)
            pool.wait_ge(consts, 10)
            for c in range(NS):
                for t, base, step in ((0, c * P + 1, 1), (1, S - c * P, -1), (2, S - 1, 0)):
                    nc.gpsimd.iota(cnt_t[:, t, c:c + 1], pattern=[[0, 1]], base=base, channel_multiplier=step,
                                   allow_small_or_imprecise_dtypes=True)
            nc.gpsimd.memset(x1[:, :, :, D:DZ], 1.0).then_inc(consts, 1)
            pool.wait_ge(consts, NCONST)

            def mask_part(n):
                c, t = n // NT, n % NT
                compare, base, step = ((ALU.is_ge, -c * P, 1), (ALU.is_ge, c * P, -1), (ALU.not_equal, c * P, -1))[t]
                nc.gpsimd.affine_select(out=mask[:, t, c, :], in_=mask[:, t, c, :], compare_op=compare, fill=NEG,
                                        base=base, pattern=[[step, S]], channel_multiplier=-step).then_inc(mask_ready, 1)

            def select(i, u):
                b = i + u
                lang = pool.value_load(of(ids_i[0:1, 0, :], i, u), min_val=0, max_val=L - 1)
                if isinstance(i, int) and b == 0:
                    pool.wait_ge(wall_ready, 3)
                if reused(i, u, V):
                    pool.wait_ge(projected, b - V + 1)
                nc.gpsimd.tensor_copy(wsel[:, u % V, :, :], wall[:, bass.ds(lang, 1), :, :].rearrange("p a c n -> p (a c) n")
                                      ).then_inc(w_selected, 1)
                if u % 2 == 0:
                    if reused(i, u, 2 * V):
                        pool.wait_ge(scored, b - 2 * V + 2)
                    pool.wait_ge(w_selected, b + 1)
                    nc.gpsimd.tensor_copy(v_row[:, u // 2 % V, :], v_hot[:].rearrange("p k n -> p (k n)")[:, bass.ds(b * (B // 2), B)]
                                          ).then_inc(v_selected, 2)
                if isinstance(i, int) and i == 0 and u < NT * NS:
                    mask_part(u)

            pool.wait_ge(more_loaded, 16 * N_MORE)
            over(pool, select)

            def low_y(i, u):
                b = i + u
                if isinstance(i, int) and b == 0:
                    return
                pool.wait_ge(yh_ready, b + 1)
                if reused(i, u, V):
                    pool.wait_ge(pooled, b - V + 1)
                nc.gpsimd.tensor_tensor(yl[:, u % V, :, :], y[:, u % V, :, :], yh[:, u % V, :, :].bitcast(fp32), ALU.subtract
                                        ).then_inc(yl_ready, 1)

            over(pool, low_y)

        @block.tensor
        def _(pe):
            def transpose(i, u):
                b = i + u
                pe.wait_ge(x_loaded[u % U], i * (16 // U) + 16 * (u // U + 1))
                if reused(i, u, 2):
                    pe.wait_ge(xT_ready, b - 1)
                for c in range(ND):
                    for s in range(NS):
                        last = nc.tensor.transpose(xT_ps[u % 2][:, c * S + s * P:c * S + (s + 1) * P],
                                                   x_in[:, u % U, s, c * P:(c + 1) * P], ident[:])
                last.then_inc(transposed, 1)

            def project(i, u):
                b = i + u
                pe.wait_ge(xT_ready, b + 1)
                pe.wait_ge(w_selected, b + 1)
                if reused(i, u, 2):
                    pe.wait_ge(tanh_ready, b - 1)
                    pe.wait_ge(t_ready, b - 1)
                for c in range(ND):
                    last = nc.tensor.matmul(proj_ps[u % 2][0:M, 0:S], wsel[:, u % V, c, :],
                                            xT[:, u % 2, c, :], start=(c == 0), stop=(c == ND - 1))
                last.then_inc(projected, 1)

            def expand(i, u):
                b = i + u
                pe.wait_ge(t_ready, b + 1)
                pe.wait_ge(b_selected, b + 1)
                if reused(i, u, 2):
                    pe.wait_ge(x1_ready, b - 1)
                for s in range(NS):
                    last = nc.tensor.matmul(lora_ps[u % 2][:, s * D:(s + 1) * D], tT[T0:K, u % V, s * P:(s + 1) * P],
                                            wselB[T0:K, u % V, :], start=True, stop=True)
                last.then_inc(lora_done, 1)

            def score(i, u):
                b = i + u
                pe.wait_ge(tanh_ready, b + 1)
                pe.wait_ge(v_selected, b + 1)
                first, final = (isinstance(i, int) and i + u == n for n in (1, B - 1))
                nc.tensor.matmul(score_ps[0:B, 0:S], v_row[:, u // 2 % V, :], tanh[:, u // 2 % V, :],
                                 start=first, stop=final).then_inc(scored, 2)

            def keep_warm(n):
                for _ in range(n):
                    nc.tensor.matmul(bank[6][:, 0:P], ident[:], ones[:], start=True, stop=True)

            W = work_ps
            pe.wait_ge(ident_ready, 1)
            keep_warm(9)
            pe.wait_ge(core_loaded, 16 * N_CORE)
            pe.wait_ge(ident_ready, 3)
            for c in range(ND):
                nc.tensor.matmul(W[0:L * R, 192:192 + A], lB[:, c * L:(c + 1) * L, :].rearrange("p l r -> p (l r)"), w1[:, c, :],
                                 start=(c == 0), stop=(c == ND - 1))
            for c in range(ND):
                nc.tensor.transpose(bank[1][:, 64 * c:64 * c + L * R], lAn[:, c * P:(c + 1) * P], ident[0:L * R, 0:L * R])
                last = nc.tensor.transpose(W[:, 128 + L * c:128 + L * (c + 1)], emb[:, c * P:(c + 1) * P], ident[0:L, 0:L])
            last.then_inc(small_T, 1)
            keep_warm(2)
            pe.wait_ge(G_ready, 1)
            for c in range(ND):
                nc.tensor.matmul(bank[2 + c][:, 0:L * A], lAn[:, c * P:(c + 1) * P],
                                 G[:].rearrange("k l a -> k (l a)"), start=True, stop=True).then_inc(folded, 1)
            transpose(0, 0)
            pe.wait_ge(more_loaded, 16 * N_MORE)
            pe.wait_ge(lBx_ready, 1)
            for c in range(ND):
                nc.tensor.matmul(bank[6][0:L, B:B + A], embT[:, c * L:(c + 1) * L], w1[:, c, :], start=(c == 0), stop=False)
            nc.tensor.matmul(bank[6][0:L, B:B + A], ones[0:1, 0:L], b1r[:], start=False, stop=True).then_inc(bias_L, 1)
            for l in range(L):
                for c in range(ND):
                    last = nc.tensor.transpose(bank[4 + l // 2][:, (l % 2) * D + c * P:(l % 2) * D + (c + 1) * P],
                                               lBx[:, c * L + l, :], ident[:])
            last.then_inc(B_T, 1)
            pe.wait_ge(bias_L, 2)
            nc.tensor.matmul(bank[6][0:A, 0:B], biasL[:], lang_hot[:], start=True, stop=True).then_inc(bias_L, 1)

            pe.wait_ge(wall_ready, 3)

            def step(i, u):
                if exists(i, u + 1):
                    transpose(i, u + 1)
                project(i, u)
                if exists(i, u - 2):
                    expand(i, u - 2)
                    if u % 2 == 1:
                        score(i, u - 2)

            over(pe, step)
            score(B - U, U - 1)
            expand(B - U, U - 2)

            pe.wait_ge(s_row_ready, 1)
            for s in range(NS):
                last = nc.tensor.transpose(work_ps[:, s * B:(s + 1) * B], s_row[:, s * P:(s + 1) * P], ident[0:B, 0:B])
            last.then_inc(s_col_done, 1)
            keep_warm(16)
            pe.wait_ge(mask_ready, NT * NS)
            pe.wait_ge(pick_ready, U)

            def argument(i, u):
                b = i + u
                kind = pe.value_load(of(ids_i[0:1, 1, :], i, u), min_val=0, max_val=NT - 1)
                if isinstance(i, int) and b == 0:
                    pe.wait_ge(max_ready, 1)
                if reused(i, u, 2):
                    pe.wait_ge(q_ready, b - 1)
                nc.tensor.matmul(arg_ps[u % 2][:, :], identb[:],
                                 mask[:, bass.ds(kind, 1), :, :].rearrange("p a c n -> p (a c n)"),
                                 start=True, stop=False)
                for s in range(NS):
                    last = nc.tensor.matmul(arg_ps[u % 2][:, s * S:(s + 1) * S],
                                            of(pick, i, u).rearrange("p a n -> p (a n)"),
                                            parts[:], start=False, stop=(s == NS - 1))
                last.then_inc(arg_ready, 1)

            def pool_rows(i, u):
                b = i + u
                pe.wait_ge(q_ready, b + 1)
                if isinstance(i, int) and b == 0:
                    pe.wait_ge(yl0_ready, 1)
                else:
                    pe.wait_ge(yl_ready, b)
                for j in range(NS):
                    if reused(i, u, 2):
                        pe.wait_ge(o_ready[j], b - 1)
                    for s in range(NS):
                        for k, part_y in enumerate((yh, yl)):
                            last = nc.tensor.matmul(pool_ps[u % 2][:, j, 0:DZ], q[:, u % V, s, j * P:(j + 1) * P],
                                                    part_y[:, u % V, s, :], start=(s + k == 0), stop=(s + k == NS))
                last.then_inc(pooled, 1)

            argument(0, 0)
            argument(0, 1)

            def row_step(i, u):
                if exists(i, u + 2):
                    argument(i, u + 2)
                pool_rows(i, u)
                if isinstance(i, int) and i + u == 0:
                    expand(B - U, U - 1)

            over(pe, row_step)

        @block.scalar
        def _(act):
            for dst, src in (
                (lAn[:], lora_A.rearrange("l r d -> (l r) d")),
                (emb[:], lang_embed),
            ):
                act.dma_start(dst, src).then_inc(core_loaded, 16)
            act.wait_ge(consts, 1)
            nc.scalar.activation(spare[:], ones[:, 0:1], ACT.Tanh)
            for h in range(2):
                act.dma_start(v_sb[h * A:(h + 1) * A, :], v.rearrange("(a o) -> a o", o=1)).then_inc(v_loaded, 16)
            for dst, src in (
                (b1r[:], b1.rearrange("(o a) -> o a", o=1)),
                (type_i[:], prompt_type.rearrange("(n a) -> n a", a=1)),
            ):
                act.dma_start(dst, src).then_inc(more_loaded, 16)
            def copy_xT(i, u):
                b = i + u
                act.wait_ge(transposed, b + 1)
                if reused(i, u, 2):
                    act.wait_ge(projected, b - 1)
                nc.scalar.copy(xT[:, u % 2, :, :].rearrange("p c n -> p (c n)"), xT_ps[u % 2][:]).then_inc(xT_ready, 1)

            act.wait_ge(small_T, 1)
            for k in range(REP):
                last = nc.scalar.copy(wall[:, :, :, A + k * R:A + (k + 1) * R],
                                      bank[1][:, 0:128].rearrange("p (c l r) -> p l c r", c=ND, l=L))
            last.then_inc(wall_ready, 1)
            copy_xT(0, 0)
            act.wait_ge(B_T, 1)
            nc.scalar.copy(hB[:, 0:2 * D], bank[4][:]).then_inc(hB_ready, 1)
            act.wait_ge(bias_L, 3)
            nc.scalar.copy(bias[:], bank[6][0:A, 0:B]).then_inc(bias_ready, 1)
            copy_xT(0, 1)
            act.wait_ge(rB_ready, 1)
            nc.scalar.copy(hB[:, 2 * D:4 * D], bank[5][:]).then_inc(hB_ready, 1)
            act.wait_ge(bias_ready, 1)

            def high_t(i, u):
                b = i + u
                act.wait_ge(projected, b + 1)
                if reused(i, u, V):
                    act.wait_ge(lora_done, b - V + 1)
                nc.scalar.copy(tT[T0:M, u % V, :], proj_ps[u % 2][T0:M, 0:S]).then_inc(th_ready, 1)

            def squash(i, u):
                b = i + u
                act.wait_ge(projected, b + 1)
                if reused(i, u, 2 * V):
                    act.wait_ge(scored, b - 2 * V + 2 - u % 2)
                nc.scalar.activation(tanh[u % 2 * A:(u % 2 + 1) * A, u // 2 % V, :], proj_ps[u % 2][0:A, 0:S], ACT.Tanh,
                                     bias=of(bias, i, u)).then_inc(tanh_ready, 1)

            def step(i, u):
                if exists(i, u + 1) and not (isinstance(i, int) and i + u == 0):
                    copy_xT(i, u + 1)
                if isinstance(i, int) and i + u == B - 1:
                    squash(i, u)
                    high_t(i, u)
                else:
                    high_t(i, u)
                    squash(i, u)

            over(act, step)
            act.wait_ge(f_ready, 1)
            nc.scalar.activation(g_col[:], f_col[:], ACT.Exp).then_inc(g_ready, 1)
            act.wait_ge(g_ready, 1)

            def weigh_odd(i, u):
                b = i + u
                if reused(i, u, V):
                    act.wait_ge(yl_ready, b - V)
                if isinstance(i, int) and i + u == B - 3:
                    act.wait_ge(x1_ready, B)
                nc.scalar.activation(y[:, u % V, 1, :], of(x1[:, :, 1, :], i, u).rearrange("p a d -> p (a d)"),
                                     ACT.Copy, scale=of(g_col[:, 1, :], i, u)).then_inc(y_odd, 2)

            def high_y(i, u):
                b = i + u
                if u % 2 == 1:
                    act.wait_ge(y_odd, b + 1)
                act.wait_ge(y_ready, b)
                if reused(i, u, V):
                    act.wait_ge(pooled, b - V + 1)
                nc.scalar.copy(yh[:, u % V, :, :], y[:, u % V, :, :]).then_inc(yh_ready, 1)

            def powers(i, u):
                b = i + u
                act.wait_ge(arg_ready, b + 1)
                if reused(i, u, V):
                    act.wait_ge(pooled, b - V + 1)
                for s in range(NS):
                    last = nc.scalar.activation(q[:, u % V, s, :], arg_ps[u % 2][:, s * S:(s + 1) * S], ACT.Exp,
                                                bias=of(q_bias[:, s, :], i, u), scale=LN2)
                last.then_inc(q_ready, 1)

            for s in range(NS):
                last = nc.scalar.activation(yh[:, 0, s, :], x1[:, 0, s, :], ACT.Copy, scale=g_col[:, s, 0:1])
            last.then_inc(yh_ready, 1)
            weigh_odd(0, 1)
            high_y(0, 1)
            powers(0, 0)
            high_y(0, 2)
            powers(0, 1)
            weigh_odd(0, 3)

            def row_step(i, u):
                if exists(i, u + V) and u % 2 == 1:
                    weigh_odd(i, u + V)
                if exists(i, u + 2):
                    powers(i, u + 2)
                if exists(i, u + 3):
                    high_y(i, u + 3)

            over(act, row_step)

        @block.vector
        def _(dve):
            chain = [0]

            def link(ins):
                chain[0] += 1
                ins.then_inc(link_d, 1)
                dve.wait_ge(link_d, chain[0])

            W = work_ps
            nc.vector.memset(tT[T0:P, :, :].bitcast(fp32), 1.0)
            nc.vector.memset(pre[:, 0:1], -BIG)
            nc.vector.memset(suf[:, S:S + 1], -BIG)
            link(nc.vector.memset(lBx[:], 0.0))
            dve.wait_ge(ident_ready, 2)
            nc.vector.tensor_tensor(picked[:], ident[:, 0:B], ident[:, B:2 * B], ALU.add)
            dve.wait_ge(core_loaded, 16 * N_CORE)
            for k in range(REP):
                nc.vector.tensor_copy(lBx[:, :, T0 + k * R:T0 + (k + 1) * R], lB[:])
            dve.wait_ge(small_T, 1)
            dve.wait_ge(ident_ready, 3)
            nc.vector.tensor_tensor(G[:], W[0:L * R, 192:192 + A].rearrange("p (l a) -> p l a", l=1).to_broadcast([L * R, L, A]),
                                    own[:].rearrange("p (l a) -> p l a", a=1).to_broadcast([L * R, L, A]), ALU.mult
                                    ).then_inc(G_ready, 1)
            link(nc.vector.tensor_copy(embT[:], W[:, 128:128 + ND * L]))
            nc.vector.tensor_copy(lBx[:, :, M:K], embT[:].rearrange("p (k a) -> p k a", a=1).to_broadcast([P, L * ND, 2])
                                  ).then_inc(lBx_ready, 1)
            for c in range(ND):
                dve.wait_ge(folded, c + 1)
                nc.vector.tensor_tensor(wall[:, :, c, 0:A], bank[2 + c][:, 0:L * A].rearrange("p (l a) -> p l a", l=L),
                                        w1[:, c:c + 1, :].to_broadcast([P, L, A]), ALU.add).then_inc(wall_ready, 1)
            dve.wait_ge(more_loaded, 16 * N_MORE)
            link(nc.vector.tensor_copy(ids[:], ids_i[:]))
            dve.wait_ge(bias_L, 1)
            nc.vector.tensor_copy(biasL[:], bank[6][0:L, B:B + A])
            dve.wait_ge(consts, 8)
            nc.vector.tensor_scalar(lang_hot[:], ids[0:L, 0, :], part[0:L, :], None, ALU.is_equal).then_inc(bias_L, 1)
            dve.wait_ge(B_T, 1)
            nc.vector.tensor_scalar(rB[:, 2 * D:4 * D], bank[5][:], low[:], None, ALU.mult).then_inc(rB_ready, 1)
            dve.wait_ge(hB_ready, 1)
            nc.vector.tensor_scalar(rB[:, 0:2 * D], bank[4][:], low[:], None, ALU.mult).then_inc(rB_ready, 1)
            dve.wait_ge(hB_ready, 2)
            dve.wait_ge(rB_ready, 2)
            nc.vector.scalar_tensor_tensor(wallB[:].rearrange("p l d -> p (l d)"), hB[:].bitcast(fp32),
                                           sign[:], rB[:], ALU.mult, ALU.add).then_inc(wallB_ready, 1)

            def types(part_of_it):
                if part_of_it == 0:
                    nc.vector.tensor_copy(type_r[:], type_i[:])
                    for t in range(NT):
                        last = nc.vector.tensor_single_scalar(hot[:, t, :], ids[:, 1, :], float(t), op=ALU.is_equal)
                    link(last)
                elif part_of_it == 1:
                    for t in range(NT):
                        last = nc.vector.tensor_single_scalar(hot_r[:, t:t + 1], type_r[:], float(t), op=ALU.is_equal)
                    link(last)
                    for t, forbidden in ((0, 1), (1, 0), (2, 2)):
                        last = nc.vector.tensor_scalar(cap[:, t:t + 1], hot_r[:, forbidden:forbidden + 1], -2 * BIG, BIG,
                                                       ALU.mult, ALU.add)
                    link(last)
                else:
                    t = part_of_it - 2
                    for c in range(NS):
                        if t == 0:
                            last = nc.vector.tensor_scalar(cnt[:, :, c], hot[:, t, :], cnt_t[:, t, c:c + 1], None, ALU.mult)
                        else:
                            last = nc.vector.scalar_tensor_tensor(cnt[:, :, c], hot[:, t, :], cnt_t[:, t, c:c + 1],
                                                                  cnt[:, :, c], ALU.mult, ALU.add)
                    link(last)

            def pick_part(n):
                group = slice(n * B // U, (n + 1) * B // U)
                nc.vector.tensor_scalar(pick[:, group, :], picked[:, group].rearrange("p (b a) -> p b a", a=1
                                                                                      ).to_broadcast([P, B // U, P]),
                                        -1.0, None, ALU.mult).then_inc(pick_ready, 1)

            def select_B(i, u):
                b = i + u
                lang = dve.value_load(of(ids_i[0:1, 0, :], i, u), min_val=0, max_val=L - 1)
                if reused(i, u, V):
                    dve.wait_ge(lora_done, b - V + 1)
                nc.vector.tensor_copy(wselB[:, u % V, :], wallB[:, bass.ds(lang, 1), :].rearrange("p a n -> p (a n)")
                                      ).then_inc(b_selected, 1)

            dve.wait_ge(wallB_ready, 1)

            def low_t(i, u):
                b = i + u
                dve.wait_ge(th_ready, b + 1)
                nc.vector.tensor_tensor(tT[TL:M, u % V, :], proj_ps[u % 2][TL:M, 0:S], tT[TL:M, u % V, :].bitcast(fp32),
                                        ALU.subtract).then_inc(t_ready, 1)

            def add_lora(i, u):
                b = i + u
                dve.wait_ge(lora_done, b + 1)
                nc.vector.tensor_tensor(of(x1[:, :, :, 0:D], i, u).rearrange("p a c d -> p (a c) d"),
                                        lora_ps[u % 2][:].rearrange("p (c d) -> p c d", c=NS),
                                        x_in[:, u % U, :, :], ALU.add).then_inc(x1_ready, 1)

            def step(i, u):
                if isinstance(i, int) and i + u == B - 1:
                    return
                low_t(i, u)
                select_B(i, u)
                if isinstance(i, int) and i == 0 and 2 <= u < 2 + NT + 2:
                    types(u - 2)
                elif isinstance(i, int) and (i > 0 or u == U - 1):
                    pick_part(u)
                if exists(i, u - 2):
                    add_lora(i, u - 2)

            dve.wait_ge(consts, NCONST)
            over(dve, step)

            def weigh(i, u, s):
                ins = nc.vector.tensor_scalar(y[:, u % V, s, :], of(x1[:, :, s, :], i, u).rearrange("p a d -> p (a d)"),
                                              of(g_col[:, s, :], i, u), None, ALU.mult)
                if s == NS - 1 or u % 2 == 1:
                    ins.then_inc(y_ready, 1)

            dve.wait_ge(scored, B)
            row, col = link_row, link_col
            nc.vector.tensor_scalar(n_row[:], score_ps[0:B, 0:S], LOG2E, ROUND, ALU.mult, ALU.add).then_inc(row, 1)
            nc.vector.tensor_copy(s_row[:], score_ps[0:B, 0:S]).then_inc(s_row_ready, 1)
            dve.wait_ge(row, 1)
            nc.vector.tensor_scalar(n_row[:], n_row[:], ROUND, None, ALU.subtract).then_inc(row, 1)
            dve.wait_ge(row, 2)
            nc.vector.tensor_tensor_scan(pre[:, 1:S + 1], n_row[:], cap[:, 0:1].to_broadcast([B, S]), -BIG, ALU.max, ALU.min
                                         ).then_inc(row, 1)
            dve.wait_ge(s_col_done, 1)
            nc.vector.tensor_copy(s_col[:].rearrange("p s b -> p (s b)"), work_ps[:, 0:NS * B]).then_inc(col, 1)
            nc.vector.tensor_tensor_scan(suf[:, S - 1::-1], n_row[:, ::-1], cap[:, 1:2].to_broadcast([B, S]), -BIG, ALU.max, ALU.min
                                         ).then_inc(row, 1)
            dve.wait_ge(col, 1)
            nc.vector.tensor_scalar(n_col[:], s_col[:], LOG2E, ROUND, ALU.mult, ALU.add).then_inc(col, 1)
            dve.wait_ge(row, 4)
            nc.vector.tensor_tensor(m[:, 0, :], pre[:, 0:S], suf[:, 1:S + 1], ALU.max).then_inc(row, 1)
            dve.wait_ge(col, 2)
            nc.vector.tensor_scalar(n_col[:], n_col[:], ROUND, None, ALU.subtract).then_inc(col, 1)
            dve.wait_ge(col, 3)
            nc.vector.scalar_tensor_tensor(f_col[:], n_col[:], -LN2_HI, s_col[:], ALU.mult, ALU.add).then_inc(col, 1)
            nc.vector.tensor_scalar(q_bias[:], n_col[:], LN2, NUDGE, ALU.mult, ALU.add)
            dve.wait_ge(col, 4)
            nc.vector.scalar_tensor_tensor(f_col[:], n_col[:], -LN2_LO, f_col[:], ALU.mult, ALU.add).then_inc(f_ready, 1)
            dve.wait_ge(row, 5)
            nc.vector.scalar_tensor_tensor(m[:, 1, :], n_row[:], cap[:, 2:3], m[:, 0, :], ALU.min, ALU.max).then_inc(row, 1)
            dve.wait_ge(row, 6)
            nc.vector.tensor_copy(parts[0:B, :], m[:, 1, :]).then_inc(row, 1)
            dve.wait_ge(row, 7)
            nc.vector.tensor_tensor(parts[B:2 * B, :], m[:, 1, :], parts[0:B, :], ALU.subtract).then_inc(max_ready, 1)
            dve.wait_ge(g_ready, 1)
            weigh(0, 1, 0)
            low_t(B - U, U - 1)
            dve.wait_ge(yh_ready, 1)
            for s in range(NS):
                last = nc.vector.scalar_tensor_tensor(yl[:, 0, s, :], x1[:, 0, s, :], g_col[:, s, 0:1],
                                                      yh[:, 0, s, :].bitcast(fp32), ALU.mult, ALU.subtract)
            last.then_inc(yl0_ready, 1)
            weigh(0, 2, 0)
            weigh(0, 2, 1)
            weigh(0, 3, 0)
            select_B(B - U, U - 1)
            add_lora(B - U, U - 3)
            add_lora(B - U, U - 2)

            def output(i, u):
                b = i + u
                k = u % 2
                if reused(i, u, V):
                    dve.wait_ge(stored[u % V], i * (16 // V) + 16 * (u // V))
                dve.wait_ge(pooled, b + 1)
                nc.vector.tensor_tensor(zc[:, k, :], pool_ps[k][:, :, D], of(cnt, i, u).rearrange("p a c -> p (a c)"),
                                        ALU.mult).then_inc(z_ready, 1)
                if exists(i, u + V):
                    weigh(i, u + V, 0)
                dve.wait_ge(z_ready, b + 1)
                nc.vector.reciprocal(rz[:, k, :], zc[:, k, :]).then_inc(r_ready, 1)
                if exists(i, u + V) and u % 2 == 0:
                    weigh(i, u + V, 1)
                dve.wait_ge(r_ready, b + 1)
                for j in range(NS):
                    nc.vector.scalar_tensor_tensor(o[:, u % V, j, :], pool_ps[k][:, j, 0:D], rz[:, k, j:j + 1],
                                                   of(x1[:, :, j, 0:D], i, u).rearrange("p a d -> p (a d)"),
                                                   ALU.mult, ALU.add).then_inc(o_ready[j], 1)

            def row_step(i, u):
                output(i, u)
                if isinstance(i, int) and i + u == 1:
                    add_lora(B - U, U - 1)

            over(dve, row_step)


NCONST = 11

_INS = ['x', 'itok_B_0_2', 'itok_B_0_3', 'L0_cond_lora_A', 'L0_cond_lora_B', 'L0_cond_lang_embed',
        'L1_cond_W1', 'L1_cond_b1', 'L1_cond_v']


def kernel(**inputs):
    import numpy as _np
    import concourse.bacc as _bacc
    from concourse import mybir as _mybir
    from concourse.bass_utils import run_bass_kernel_spmd as _run

    nc = _bacc.Bacc("TRN2", target_bir_lowering=False, num_devices=1)
    arrays, args = {}, []
    for name in _INS:
        a = _np.ascontiguousarray(inputs[name])
        arrays[f"in_{name}"] = a
        args.append(nc.dram_tensor(f"in_{name}", a.shape, _mybir.dt.from_np(a.dtype), kind="ExternalInput").ap())
    out = nc.dram_tensor("out", inputs["x"].shape, _mybir.dt.float32, kind="ExternalOutput").ap()
    lora_prompt_pool_kernel(nc, *args, out)
    r = _run(nc, [arrays], core_ids=[0])
    return r.results[0]["out"]
```
